# Optimizing a Trainium2 kernel written in Bass

```python
import numpy as np
import jax
import jax.numpy as jnp

def _softmax(x, axis=-1):
    return jax.nn.softmax(x, axis=axis)

def _gelu(x):
    return jax.nn.gelu(x, approximate=True)

def _silu(x):
    return jax.nn.silu(x)

def _sigmoid(x):
    return jax.nn.sigmoid(x)

def _layernorm(x, axis=-1, eps=1e-05):
    m = jnp.mean(x, axis=axis, keepdims=True)
    v = jnp.var(x, axis=axis, keepdims=True)
    return (x - m) / jnp.sqrt(v + eps)

def _scatter_add(tgt, idx, src, axis=0):
    return tgt.at[idx].add(src)

def _segment_sum(src, seg, n):
    return jax.ops.segment_sum(src, seg, n)
kernel_name = 'mk_flamingo_gated_d2_seqx_r4_61b352'

def setup_inputs(seed: int=0):
    np.random.seed(seed)
    _w = jnp.asarray

    def _rec_inputs():
        import jax
        import jax.numpy as jnp
        _rk = jax.random.key(seed)
        x = 7.22e-05 + 1 * jax.random.normal(jax.random.fold_in(_rk, 1), (4, 512, 512), jnp.float32)
        _lenS = 512 - jax.random.randint(jax.random.fold_in(_rk, 7), (4,), 0, max(1, 512 // 4) + 1, jnp.int32)
        _lenS2 = 512 - jax.random.randint(jax.random.fold_in(_rk, 8), (4,), 0, max(1, 512 // 4) + 1, jnp.int32)
        _ctx_1024P = jax.random.normal(jax.random.fold_in(_rk, 11), (4, 16, 256), jnp.float32)
        _ctx_1024c = jax.random.dirichlet(jax.random.fold_in(_rk, 511), 0.3 * jnp.ones((16,), jnp.float32), (4, 512))
        _ctx_1024t = jnp.einsum('bsk,bkd->bsd', _ctx_1024c, _ctx_1024P)
        _ctx_1024t = _ctx_1024t * jax.lax.rsqrt(jnp.mean(jnp.square(_ctx_1024t)) + 1e-12) * 0.953939
        ctx_1024 = 2.81802e-05 + 1.00001 * (_ctx_1024t + 0.3 * jax.random.normal(jax.random.fold_in(_rk, 611), (4, 512, 256), jnp.float32))
        _g = jax.random.normal(jax.random.fold_in(_rk, 9001), (2, 2), jnp.float32)
        _g = jnp.sign(_g) * jnp.maximum(jnp.abs(_g), 1.0) + (_g == 0) * 1.0
        g_xattn = _g[0]
        g_ffn = _g[1]
        return (x, ctx_1024, g_xattn, g_ffn)
    x, ctx_1024, g_xattn, g_ffn = _rec_inputs()

    def _L0_xattn_setup():
        import jax, jax.numpy as jnp
        import numpy as np
        key = jax.random.key(seed)
        ks = jax.random.split(key, 6)
        B, L, N, C, D = (8, 128, 512, 256, 128)
        return {'teacher_logits': jax.random.normal(ks[0], (B, L, N), dtype=jnp.float32), 'teacher_features': jax.random.normal(ks[1], (B, N, C), dtype=jnp.float32), 'Wq': jax.random.normal(ks[2], (D, C), dtype=jnp.float32) * (1.0 / np.sqrt(C)), 'bq': jnp.zeros((D,), dtype=jnp.float32), 'Wk': jax.random.normal(ks[3], (D, C), dtype=jnp.float32) * (1.0 / np.sqrt(C)), 'bk': jnp.zeros((D,), dtype=jnp.float32)}
    _L0_xattn_all = _L0_xattn_setup()
    _L0_xattn_in = {k: v for k, v in _L0_xattn_all.items() if k in ('Wq', 'bq', 'Wk', 'bk')}
    del _L0_xattn_all

    def _L0_ffn_setup():
        import jax, jax.numpy as jnp
        import numpy as np
        NBITS = 4
        OUT_F = 512
        IN_F = 512

        def _bit_ste(w, nbits):
            step = float(2 ** nbits - 1)
            w = jnp.clip(w, -1.0, 1.0)
            return jnp.round(jnp.abs(w) * step) / step * jnp.sign(w)
        key = jax.random.key(seed)
        ks = jax.random.split(key, 6)
        ex = np.arange(NBITS - 1, -1, -1)
        exps = jnp.asarray(2.0 ** ex / (2.0 ** NBITS - 1), dtype=jnp.float32)
        inp = {'input': jax.random.normal(ks[0], (8, 512, IN_F), dtype=jnp.float32), 'pweight': jax.random.normal(ks[1], (OUT_F, IN_F, NBITS), dtype=jnp.float32), 'nweight': jax.random.normal(ks[2], (OUT_F, IN_F, NBITS), dtype=jnp.float32), 'exps': exps, 'bexps': exps, 'mask_weight': jnp.ones((NBITS,), dtype=jnp.float32), 'scale': jnp.array([0.05], dtype=jnp.float32), 'pbias': jax.random.uniform(ks[3], (OUT_F, NBITS), dtype=jnp.float32, minval=0.0, maxval=float(2 ** NBITS - 1)) // 1.0 % 2.0, 'nbias': jax.random.uniform(ks[4], (OUT_F, NBITS), dtype=jnp.float32, minval=0.0, maxval=float(2 ** NBITS - 1)) // 1.0 % 2.0, 'biasscale': jnp.array([0.05], dtype=jnp.float32)}
        return inp
    _L0_ffn_all = _L0_ffn_setup()
    _L0_ffn_in = {k: v for k, v in _L0_ffn_all.items() if k in ('pweight', 'nweight', 'exps', 'bexps', 'mask_weight', 'scale', 'pbias', 'nbias', 'biasscale')}
    del _L0_ffn_all

    def _L1_xattn_setup():
        import jax, jax.numpy as jnp
        import numpy as np
        EPS = 1e-05

        def rmsnorm(x, g, eps=EPS):
            var = jnp.mean(jnp.square(x), axis=-1, keepdims=True)
            return x * jax.lax.rsqrt(var + eps) * g
        key = jax.random.key(seed)
        ks = jax.random.split(key, 8)
        B, Sq, Skv = (2, 1024, 128)
        dim, cdim, H, D = (512, 256, 16, 128)
        inner = H * D
        s = lambda f: 1.0 / np.sqrt(f)
        return {'hidden_states': jax.random.normal(ks[0], (B, Sq, dim), jnp.float32), 'encoder_hidden_states': jax.random.normal(ks[1], (B, Skv, cdim), jnp.float32), 'Wq': jax.random.normal(ks[2], (dim, inner), jnp.float32) * s(dim), 'Wk': jax.random.normal(ks[3], (cdim, inner), jnp.float32) * s(cdim), 'Wv': jax.random.normal(ks[4], (cdim, inner), jnp.float32) * s(cdim), 'Wo': jax.random.normal(ks[5], (inner, dim), jnp.float32) * s(inner), 'gq': jnp.ones((D,), jnp.float32), 'gk': jnp.ones((D,), jnp.float32)}
    _L1_xattn_all = _L1_xattn_setup()
    _L1_xattn_in = {k: v for k, v in _L1_xattn_all.items() if k in ('Wq', 'Wk', 'Wv', 'Wo', 'gq', 'gk')}
    del _L1_xattn_all

    def _L1_ffn_setup():
        import jax, jax.numpy as jnp
        import numpy as np
        E, H, I, TOPK = (16, 512, 352, 4)
        B, S = (2, 256)
        key = jax.random.key(seed)
        ks = jax.random.split(key, 6)
        hidden_states = jax.random.normal(ks[0], (B, S, H), dtype=jnp.float32)
        topk_idx = jax.random.randint(ks[1], (B, S, TOPK), 0, E)
        topk_weight = jax.random.uniform(ks[2], (B, S, TOPK), dtype=jnp.float32) / TOPK
        gate_weight = jax.random.normal(ks[3], (E, I, H), dtype=jnp.float32) * (1.0 / np.sqrt(H))
        up_weight = jax.random.normal(ks[4], (E, I, H), dtype=jnp.float32) * (1.0 / np.sqrt(H))
        down_weight = jax.random.normal(ks[5], (E, H, I), dtype=jnp.float32) * (1.0 / np.sqrt(I))
        return {'hidden_states': hidden_states, 'topk_idx': topk_idx, 'topk_weight': topk_weight, 'gate_weight': gate_weight, 'up_weight': up_weight, 'down_weight': down_weight}
    _L1_ffn_all = _L1_ffn_setup()
    _L1_ffn_in = {k: v for k, v in _L1_ffn_all.items() if k in ('topk_idx', 'topk_weight', 'gate_weight', 'up_weight', 'down_weight')}
    del _L1_ffn_all
    return {'x': x, 'ctx_1024': ctx_1024, 'g_xattn': g_xattn, 'g_ffn': g_ffn, 'L0_xattn_Wq': _L0_xattn_in['Wq'], 'L0_xattn_bq': _L0_xattn_in['bq'], 'L0_xattn_Wk': _L0_xattn_in['Wk'], 'L0_xattn_bk': _L0_xattn_in['bk'], 'L0_ffn_pweight': _L0_ffn_in['pweight'], 'L0_ffn_nweight': _L0_ffn_in['nweight'], 'L0_ffn_exps': _L0_ffn_in['exps'], 'L0_ffn_bexps': _L0_ffn_in['bexps'], 'L0_ffn_mask_weight': _L0_ffn_in['mask_weight'], 'L0_ffn_scale': _L0_ffn_in['scale'], 'L0_ffn_pbias': _L0_ffn_in['pbias'], 'L0_ffn_nbias': _L0_ffn_in['nbias'], 'L0_ffn_biasscale': _L0_ffn_in['biasscale'], 'L1_xattn_Wq': _L1_xattn_in['Wq'], 'L1_xattn_Wk': _L1_xattn_in['Wk'], 'L1_xattn_Wv': _L1_xattn_in['Wv'], 'L1_xattn_Wo': _L1_xattn_in['Wo'], 'L1_xattn_gq': _L1_xattn_in['gq'], 'L1_xattn_gk': _L1_xattn_in['gk'], 'L1_ffn_topk_idx': _L1_ffn_in['topk_idx'], 'L1_ffn_topk_weight': _L1_ffn_in['topk_weight'], 'L1_ffn_gate_weight': _L1_ffn_in['gate_weight'], 'L1_ffn_up_weight': _L1_ffn_in['up_weight'], 'L1_ffn_down_weight': _L1_ffn_in['down_weight']}

def reference(x, ctx_1024, g_xattn, g_ffn, L0_xattn_Wq, L0_xattn_bq, L0_xattn_Wk, L0_xattn_bk, L0_ffn_pweight, L0_ffn_nweight, L0_ffn_exps, L0_ffn_bexps, L0_ffn_mask_weight, L0_ffn_scale, L0_ffn_pbias, L0_ffn_nbias, L0_ffn_biasscale, L1_xattn_Wq, L1_xattn_Wk, L1_xattn_Wv, L1_xattn_Wo, L1_xattn_gq, L1_xattn_gk, L1_ffn_topk_idx, L1_ffn_topk_weight, L1_ffn_gate_weight, L1_ffn_up_weight, L1_ffn_down_weight):
    import jax
    import jax.numpy as jnp

    def _L0_xattn_ref(teacher_logits, teacher_features, Wq, bq, Wk, bk):
        import jax, jax.numpy as jnp
        import numpy as np
        query = jnp.einsum('bnc,dc->bnd', teacher_features, Wq) + bq
        key = jnp.einsum('bnc,dc->bnd', teacher_features, Wk) + bk
        energy = jnp.einsum('bnd,bmd->bnm', query, key)
        attention = jax.nn.softmax(energy, axis=-1)
        x_m = jnp.einsum('bln,bmn->blm', teacher_logits, attention)
        return x_m

    def _L0_ffn_ref(input, pweight, nweight, exps, bexps, mask_weight, scale, pbias, nbias, biasscale):
        import jax, jax.numpy as jnp
        import numpy as np
        NBITS = 4
        OUT_F = 512
        IN_F = 512

        def _bit_ste(w, nbits):
            step = float(2 ** nbits - 1)
            w = jnp.clip(w, -1.0, 1.0)
            return jnp.round(jnp.abs(w) * step) / step * jnp.sign(w)
        temp = 1.0
        mask = jax.nn.sigmoid(mask_weight)
        soft = jax.nn.sigmoid(temp * pweight) - jax.nn.sigmoid(temp * nweight)
        weight = jnp.einsum('oin,n->oi', soft, exps * mask) * scale[0]
        bias_raw = jnp.einsum('on,n->o', pbias - nbias, bexps)
        bias = _bit_ste(bias_raw, NBITS) * biasscale[0]
        return jnp.einsum('bsi,oi->bso', input, weight) + bias

    def _L1_xattn_ref(hidden_states, encoder_hidden_states, Wq, Wk, Wv, Wo, gq, gk):
        import jax, jax.numpy as jnp
        import numpy as np
        EPS = 1e-05

        def rmsnorm(x, g, eps=EPS):
            var = jnp.mean(jnp.square(x), axis=-1, keepdims=True)
            return x * jax.lax.rsqrt(var + eps) * g
        B, Sq, _ = hidden_states.shape
        Skv = encoder_hidden_states.shape[1]
        D = gq.shape[0]
        H = Wq.shape[1] // D
        scale = 1.0 / np.sqrt(D)
        q = (hidden_states @ Wq).reshape(B, Sq, H, D)
        k = (encoder_hidden_states @ Wk).reshape(B, Skv, H, D)
        v = (encoder_hidden_states @ Wv).reshape(B, Skv, H, D)
        q = rmsnorm(q, gq)
        k = rmsnorm(k, gk)
        scores = jnp.einsum('bqhd,bkhd->bhqk', q, k) * scale
        attn = jax.nn.softmax(scores, axis=-1)
        out = jnp.einsum('bhqk,bkhd->bqhd', attn, v)
        out = out.reshape(B, Sq, H * D)
        return out @ Wo

    def _L1_ffn_ref(hidden_states, topk_idx, topk_weight, gate_weight, up_weight, down_weight):
        import jax, jax.numpy as jnp
        import numpy as np
        E, H, I, TOPK = (16, 512, 352, 4)
        B, S = (2, 256)
        b, s, h = hidden_states.shape
        n_tokens = b * s
        topk = topk_idx.shape[-1]
        x = hidden_states.reshape(n_tokens, h)
        flat_expert = topk_idx.reshape(-1)
        flat_weight = topk_weight.reshape(-1).astype(hidden_states.dtype)
        perm = jnp.argsort(flat_expert)
        tok = jnp.repeat(jnp.arange(n_tokens), topk)[perm]
        xs = x[tok]
        group_sizes = jnp.bincount(flat_expert, length=E).astype(jnp.int32)
        gate = jax.lax.ragged_dot(xs, jnp.swapaxes(gate_weight, 1, 2), group_sizes)
        up = jax.lax.ragged_dot(xs, jnp.swapaxes(up_weight, 1, 2), group_sizes)
        h_act = jax.nn.silu(gate) * up
        down = jax.lax.ragged_dot(h_act, jnp.swapaxes(down_weight, 1, 2), group_sizes)
        w_sorted = flat_weight[perm]
        out = jnp.zeros((n_tokens, h), hidden_states.dtype).at[tok].add(down * w_sorted[:, None])
        return out.reshape(b, s, h)
    x = x + jnp.tanh(g_xattn[0]) * _L0_xattn_ref(_layernorm(x, axis=-1), ctx_1024, L0_xattn_Wq, L0_xattn_bq, L0_xattn_Wk, L0_xattn_bk)
    x = x + jnp.tanh(g_ffn[0]) * _L0_ffn_ref(_layernorm(x, axis=-1), L0_ffn_pweight, L0_ffn_nweight, L0_ffn_exps, L0_ffn_bexps, L0_ffn_mask_weight, L0_ffn_scale, L0_ffn_pbias, L0_ffn_nbias, L0_ffn_biasscale)
    x = x + jnp.tanh(g_xattn[1]) * _L1_xattn_ref(_layernorm(x, axis=-1), ctx_1024, L1_xattn_Wq, L1_xattn_Wk, L1_xattn_Wv, L1_xattn_Wo, L1_xattn_gq, L1_xattn_gk)
    x = x + jnp.tanh(g_ffn[1]) * _L1_ffn_ref(_layernorm(x, axis=-1), L1_ffn_topk_idx, L1_ffn_topk_weight, L1_ffn_gate_weight, L1_ffn_up_weight, L1_ffn_down_weight)
    return x

_drawn_inputs = setup_inputs


def setup_inputs(seed=0):
    import zlib

    import numpy as np

    out = dict(_drawn_inputs(seed))
    spreads = {'g_ffn': (-1.0, 0.6),
     'L0_xattn_bq': (0.0, 0.1),
     'L0_xattn_bk': (0.0, 0.8),
     'L0_ffn_mask_weight': (1.0, 0.6),
     'L1_xattn_gq': (1.0, 0.565),
     'L1_xattn_gk': (1.0, 0.577)}
    factors = {'L0_ffn_bexps': 6.037, 'L0_ffn_pbias': 6.616, 'L0_ffn_nbias': 6.087}
    for name, (base, spread) in spreads.items():
        noise = np.random.default_rng([zlib.crc32(name.encode()), seed]).standard_normal(out[name].shape)
        drawn = base * np.exp(spread * noise) if base else spread * noise
        out[name] = jnp.asarray(drawn.astype(out[name].dtype))
    for name, factor in factors.items():
        out[name] = (out[name] * factor).astype(out[name].dtype)
    return out
```

```python
from contextlib import ExitStack

import concourse.bass as bass
from concourse import mybir

F32 = mybir.dt.float32
F32R = mybir.dt.float32r
I32 = mybir.dt.int32
ALU = mybir.AluOpType
ACT = mybir.ActivationFunctionType
AX_X = mybir.AxisListType.X

P = 128
B, S, D, C = 4, 512, 512, 256
NT = S // P
DT = D // P
CT = C // P
H, HD = 16, 128
NBITS = 4
E, I, TOPK = 16, 352, 4
IT = -(-I // P)
IW = [min(P, I - P * j) for j in range(IT)]
EPS = 1e-5
ROUND = 1.5 * 2.0 ** 23

BQ, BK, GQ, GK = range(4)
G_X, G_F, EXPS, BEXPS, MASK, SCALE, BSCALE = 4, 6, 8, 12, 16, 20, 21
NVEC = 22

L0_ORDER = [("K", 0), ("K", 1), ("A", 0), ("Q", 0), ("K", 2), ("A", 1), ("S", 0), ("K", 3), ("K", 4), ("G", 0), ("G", 1),
            ("P", 0), ("G", 2), ("G", 3), ("C", 0), ("Q", 1), ("S", 1), ("G", 4), ("G", 5), ("G", 6),
            ("D", 0), ("P", 1), ("G", 7), ("G", 8), ("G", 9), ("G", 10), ("A", 2), ("G", 11), ("G", 12), ("C", 1),
            ("G", 13), ("G", 14), ("G", 15), ("G", 16), ("G", 17), ("G", 18), ("G", 19), ("B", 0), ("E", 0),
            ("Q", 2), ("S", 2), ("D", 1), ("B", 1), ("F", 0), ("P", 2), ("A", 3), ("C", 2), ("E", 1), ("Q", 3), ("S", 3),
            ("D", 2), ("B", 2), ("F", 1), ("P", 3), ("C", 3), ("E", 2), ("D", 3), ("B", 3), ("F", 2), ("E", 3), ("F", 3)]
NSPLIT = 1 + B
NBIT_CHUNKS = (DT + 1) * NBITS


def numbered(kinds):
    found, n = {}, 0
    for key in L0_ORDER:
        if key[0] in kinds:
            found[key] = n
            n += 4
    return found, n


TURN, TURNS = numbered("ADFP")
XN, XNS = numbered("ADF")
WIDE, WIDES = numbered("CE")
PROB, PROBS = numbered("S")


def flamingo_kernel(nc, x, ctxT, vecs, w0, bits, w1, w_gu, w_dn, topk_idx, topk_w, out):
    x_tiles = x.rearrange("(b i p) d -> b p i d", b=B, p=P)
    out_tiles = out.rearrange("(b i p) d -> b p i d", b=B, p=P)

    with ExitStack() as ctx:
        def sb(name, shape, dt=F32):
            return ctx.enter_context(nc.sbuf_tensor(name, shape, dt))

        def sem(name):
            return ctx.enter_context(nc.semaphore(name))

        def hi_lo(name, shape):
            return [sb(f"{name}_{part}", shape, F32R) for part in ("hi", "lo")]

        def f32(ap):
            return ap.bitcast(F32)

        x_sb = sb("x_sb", [P, B, NT, D])
        xnT = hi_lo("xnT", [P, B, DT, S])
        cT = hi_lo("cT", [P, B, CT, S])
        probT = hi_lo("probT", [P, NT, S])
        kv = hi_lo("kv", [P, 2, 2, S])
        qT = hi_lo("qT", [P, 2, S])
        oT = hi_lo("oT", [P, S])
        wq = hi_lo("wq", [P, DT * HD])
        wkv = hi_lo("wkv", [P, CT, 2 * HD])
        wo = hi_lo("wo", [P, D])
        prob = sb("prob", [P, NT, S])
        xn = sb("xn", [P, NT, D])
        stage = sb("stage", [P, 4, S])
        kv_raw = sb("kv_raw", [P, NT, 2 * HD])
        sq = sb("sq", [P, S])
        ksq = sb("ksq", [P, NT, HD])
        ident = sb("ident", [P, P])
        vec = sb("vec", [P, NVEC])
        ones = sb("ones", [P, 1])
        minus_half = sb("minus_half", [P, NT])
        eps = sb("eps", [P, NT])
        tanh_g = sb("tanh_g", [P, 4])
        small = sb("small", [P, 16])
        bit_w = sb("bit_w", [P, NBITS])
        gain = sb("gain", [P, 1])
        stats = sb("stats", [P, 4, 6])
        mean_var = sb("mean_var", [P, B, NT, 2])
        var_eps = sb("var_eps", [P, NT])
        rstd = sb("rstd", [P, NT])
        neg_max = sb("neg_max", [P, 2, NT])
        neg_bias = sb("neg_bias", [P, 2, NT])
        row_sum = sb("row_sum", [P, 2, NT])
        inv_sum = sb("inv_sum", [P, 2, NT])
        q_ss = sb("q_ss", [P, 2, NT])
        q_scale = sb("q_scale", [P, 2, NT])
        k_ss = sb("k_ss", [P, NT])
        k_ms = sb("k_ms", [P, NT])
        k_rs = sb("k_rs", [P, NT])
        idx = sb("idx", [P, NT, TOPK], I32)
        idx_f = sb("idx_f", [P, NT, TOPK])
        topw = sb("topw", [P, NT, TOPK])
        picked = sb("picked", [P, NT, TOPK])
        share = sb("share", [P, NT, E])

        bias_t = kv_raw[:, 0:2, :].rearrange("p a c -> p (a c)")
        bit_acc = kv_raw[:, 2:4, :].rearrange("p a c -> p (a c)")
        w0s = oT
        wf = [t[:, :, :, :].rearrange("p a b c -> p (a b) c") for t in kv]

        s_bank = [ctx.enter_context(nc.psum_tensor(f"s_bank{i}", [P, 512], F32)) for i in range(2)]
        t_bank = [ctx.enter_context(nc.psum_tensor(f"t_bank{i}", [P, 512], F32)) for i in range(2)]
        w_bank = [ctx.enter_context(nc.psum_tensor(f"w_bank{i}", [P, 512], F32)) for i in range(2)]
        j_bank = [ctx.enter_context(nc.psum_tensor(f"j_bank{i}", [P, 512], F32)) for i in range(2)]

        vec_in, idx_in = sem("vec_in"), sem("idx_in")
        x_in = [sem(f"x_in{b}") for b in range(B)]
        chunk_in = [sem(f"chunk_in{i}") for i in range(2)]
        wq_in, wkv_in, wo_in = sem("wq_in"), sem("wkv_in"), sem("wo_in")
        gu_in, dn_in, stored = sem("gu_in"), sem("dn_in"), sem("stored")
        ident_ready, const_ready, gain_ready = sem("ident_ready"), sem("const_ready"), sem("gain_ready")
        gates_tanh, mask_tanh, bit_w_ready, share_ready = (
            sem("gates_tanh"), sem("mask_tanh"), sem("bit_w_ready"), sem("share_ready"))
        dve_own, pool_own = sem("dve_own"), sem("pool_own")
        chunk_hi, chunk_lo = sem("chunk_hi"), sem("chunk_lo")
        bit_tanh, bit_diff, bit_added = sem("bit_tanh"), sem("bit_diff"), sem("bit_added")
        wf_hi, wf_lo, bias_ready = sem("wf_hi"), sem("wf_lo"), sem("bias_ready")
        moments, xn_ready, turned, turned_hi, turned_lo = (
            sem("moments"), sem("xn_ready"), sem("turned"), sem("turned_hi"), sem("turned_lo"))
        qk0_mm, qk0_hi, qk0_lo, e0_mm, e0_max, e0_exp, e0_scaled = (
            sem("qk0_mm"), sem("qk0_hi"), sem("qk0_lo"), sem("e0_mm"), sem("e0_max"), sem("e0_exp"), sem("e0_scaled"))
        wide_mm, wide_added, bias_added = sem("wide_mm"), sem("wide_added"), sem("bias_added")
        wq_hi, wq_lo, wkv_hi, wkv_lo, wo_hi, wo_lo = (
            sem("wq_hi"), sem("wq_lo"), sem("wkv_hi"), sem("wkv_lo"), sem("wo_hi"), sem("wo_lo"))
        kv_mm, kv_copied, k_squares, k_scaled, v_hi, v_lo = (
            sem("kv_mm"), sem("kv_copied"), sem("k_squares"), sem("k_scaled"), sem("v_hi"), sem("v_lo"))
        kT_mm, kT_hi, kT_lo = sem("kT_mm"), sem("kT_hi"), sem("kT_lo")
        q_mm, q_hi, q_lo, q_squared, q_ss_mm, q_ss_out, q_scale_ready = (
            sem("q_mm"), sem("q_hi"), sem("q_lo"), sem("q_squared"), sem("q_ss_mm"), sem("q_ss_out"),
            sem("q_scale_ready"))
        s_mm, s_max, p_exp, p_turned, p_hi, p_lo = (
            sem("s_mm"), sem("s_max"), sem("p_exp"), sem("p_turned"), sem("p_hi"), sem("p_lo"))
        pv_mm, o_hi, o_lo, w_mm, w_added = sem("pv_mm"), sem("o_hi"), sem("o_lo"), sem("w_mm"), sem("w_added")
        gu_hi, gu_lo, dn_hi, dn_lo = sem("gu_hi"), sem("gu_lo"), sem("dn_hi"), sem("dn_lo")
        g_mm, u_mm, silu_ready, h_ready, h_hi, h_lo, d_mm, y_added = (
            sem("g_mm"), sem("u_mm"), sem("silu_ready"), sem("h_ready"), sem("h_hi"), sem("h_lo"), sem("d_mm"),
            sem("y_added"))

        def wait(eng, s, value):
            if isinstance(value, int) and value <= 0:
                return
            eng.wait_ge(s, value)

        def need(eng, s, per, h, k, c):
            wait(eng, s, h * (B * per) + (per * k + c))

        def need_e(eng, s, per, it, k, c):
            wait(eng, s, it * (2 * per) + (per * k + c))

        GU = 2 * DT * I
        DN = IT * D
        w_area = [t[:, 1:B, :, :].rearrange("p b j s -> p (b j s)") for t in xnT]
        c_area = [t[:, :, :, :].rearrange("p b j s -> p (b j s)") for t in cT]
        gu_w = [[w_area[part][:, slot * GU:(slot + 1) * GU] for part in range(2)] for slot in range(2)]
        dn_w = [[c_area[part][:, slot * DN:(slot + 1) * DN] for part in range(2)] for slot in range(2)]
        x_area = x_sb[:, 1:B, :, :].rearrange("p b i d -> p (b i d)")
        gu_stage, dn_stage = x_area[:, 0:GU], x_area[:, GU:GU + DN]
        hT = [[t[:, 0:IT, :] for t in probT],
              [t[:, :, :, :].rearrange("p a b s -> p (a b) s")[:, 0:IT, :] for t in kv]]

        def cols(area, which, dj, j):
            at = (which * DT + dj) * I + j * P
            return area[:, at:at + IW[j]]

        block = ctx.enter_context(nc.Block())

        @block.sync
        def _(sp):
            sp.dma_start(x_sb[:, 0, :, :], x_tiles[0]).then_inc(x_in[0], 16)
            sp.dma_start(vec[:], vecs).then_inc(vec_in, 16)

            def chunk(r):
                if r - 2 >= NSPLIT:
                    sp.wait_ge(bit_added, r - 2 - NSPLIT + 1)
                elif r >= 2:
                    sp.wait_ge(chunk_lo, r - 1)
                at = 2 * (r % 2)
                if r == 0:
                    sp.dma_start(stage[:, at, :], w0).then_inc(chunk_in[r % 2], 16)
                elif r < NSPLIT:
                    sp.dma_start(stage[:, at:at + 2, :], ctxT[r - 1].rearrange("j p s -> p j s")).then_inc(
                        chunk_in[r % 2], 16)
                else:
                    sp.dma_start(stage[:, at:at + 2, :], bits[r - NSPLIT].rearrange("w p s -> p w s")).then_inc(
                        chunk_in[r % 2], 16)

            for r in range(NSPLIT + NBIT_CHUNKS):
                chunk(r)
                if 1 <= r < B:
                    sp.dma_start(x_sb[:, r, :, :], x_tiles[r]).then_inc(x_in[r], 16)
                if r == B:
                    sp.dma_start(idx[:], topk_idx).then_inc(idx_in, 16)
                    sp.dma_start(topw[:], topk_w).then_inc(idx_in, 16)

            def head_weights(h):
                for n, (arrived, used) in enumerate(((wkv_in, wkv_lo), (wq_in, wq_lo), (wo_in, wo_lo))):
                    wait(sp, used, h)
                    src = w1[n, h] if isinstance(h, int) else w1[n, bass.ds(h, 1), :, :].rearrange("a p s -> p (a s)")
                    sp.dma_start(stage[:, n, :], src).then_inc(arrived, 16)

            sp.wait_ge(bit_added, NBIT_CHUNKS)
            head_weights(0)
            with sp.Fori(1, H) as h:
                head_weights(h)

            for b in range(1, B):
                sp.wait_ge(w_added, 4 * (B * (H - 1) + b + 1))
                sp.dma_start(out_tiles[b], x_sb[:, b, :, :]).then_inc(stored, 16)
            sp.wait_ge(stored, 16 * (B - 1))

            def expert_weights(e):
                for area, w, arrived, used in ((gu_stage, w_gu, gu_in, gu_lo), (dn_stage, w_dn, dn_in, dn_lo)):
                    wait(sp, used, e)
                    src = w[e] if isinstance(e, int) else w[bass.ds(e, 1), :, :].rearrange("a p s -> p (a s)")
                    sp.dma_start(area, src).then_inc(arrived, 16)

            expert_weights(0)
            with sp.Fori(1, E) as e:
                expert_weights(e)
            for t in range(NT):
                sp.wait_ge(y_added, NT * (E - 1) + t + 1)
                sp.dma_start(out_tiles[0][:, t, :], x_sb[:, 0, t, :]).then_inc(stored, 16)
            sp.wait_ge(stored, 16 * (B - 1 + NT))

        @block.tensor
        def _(pe):
            def product(dst, left, right, first=True, last=True):
                (lh, ll), (rh, rl) = left, right
                pe.matmul(dst, lh, rl, start=first, stop=False)
                pe.matmul(dst, lh, rh, start=False, stop=False)
                return pe.matmul(dst, ll, rh, start=False, stop=last)

            def turn(n, tile, ready, count):
                pe.wait_ge(ready, count)
                wait(pe, turned_lo, n - 1)
                for j in range(4):
                    last = pe.transpose(t_bank[n % 2][:, j * P:(j + 1) * P], tile[:, j * P:(j + 1) * P], ident[:])
                last.then_inc(turned, 1)

            pe.wait_ge(ident_ready, 2)
            for kind, b in L0_ORDER:
                if kind in "ADF":
                    for i in range(NT):
                        turn(TURN[kind, b] + i, xn[:, i, :], xn_ready, XN[kind, b] + i + 1)
                elif kind == "P":
                    for i in range(NT):
                        turn(TURN[kind, b] + i, prob[:, i, :], e0_scaled, PROB["S", b] + i + 1)
                elif kind == "Q":
                    pe.wait_ge(chunk_lo, 2 + b)
                    wait(pe, qk0_lo, 2 * b)
                    for n in range(2):
                        for cj in range(CT):
                            at = (n * CT + cj) * P
                            last = product(j_bank[n][:], [t[:, at:at + P] for t in w0s],
                                           [t[:, b, cj, :] for t in cT], cj == 0, cj == CT - 1)
                        last.then_inc(qk0_mm, 1)
                elif kind == "S":
                    pe.wait_ge(qk0_lo, 2 * (b + 1))
                    for i in range(NT):
                        wait(pe, e0_exp, PROB[kind, b] + i - 1)
                        product(s_bank[i % 2][:], [t[:, 0, i * P:(i + 1) * P] for t in qT],
                                [t[:, 1, :] for t in qT]).then_inc(e0_mm, 1)
                elif kind in "CE":
                    pe.wait_ge(turned_lo, TURN["P" if kind == "C" else "D", b] + 4)
                    if kind == "E":
                        pe.wait_ge(wf_lo, DT)
                    for i in range(NT):
                        n = WIDE[kind, b] + i
                        wait(pe, wide_added, n - 1)
                        right = probT if kind == "C" else wf
                        for j in range(DT):
                            last = product(w_bank[n % 2][:], [t[:, b, j, i * P:(i + 1) * P] for t in xnT],
                                           [t[:, j, :] for t in right], j == 0, j == DT - 1)
                        last.then_inc(wide_mm, 1)

            def step(h, k, proj=True, score=True, value=True):
                def scores(i):
                    if not score:
                        return
                    u = k - 1
                    if i == 0:
                        need(pe, q_lo, 1, h, u, 1)
                        need(pe, kT_lo, 1, h, u, 1)
                    need(pe, p_exp, 4, h, u, i - 1)
                    product(s_bank[i % 2][:], [t[:, u % 2, i * P:(i + 1) * P] for t in qT],
                            [t[:, u % 2, 0, :] for t in kv]).then_inc(s_mm, 1)

                def probs(i):
                    if not score:
                        return
                    u = k - 1
                    need(pe, p_exp, 4, h, u, i + 1)
                    if i == 0:
                        need(pe, kT_lo, 1, h, u, 1)
                    elif i == 1:
                        need(pe, p_lo, 4, h, u, 0)
                    elif i == 2:
                        need(pe, p_lo, 4, h, u, 1)
                    else:
                        need(pe, q_ss_out, 1, h, k, 1 if proj else 0)
                        need(pe, p_lo, 4, h, u, 2)
                    for j in range(4):
                        last = pe.transpose(t_bank[i % 2][:, j * P:(j + 1) * P], prob[:, i, j * P:(j + 1) * P],
                                            ident[:])
                    last.then_inc(p_turned, 1)

                def values():
                    if not value:
                        return
                    w = k - 2
                    need(pe, p_lo, 4, h, w, 4)
                    need(pe, v_lo, 1, h, w, 1)
                    need(pe, kv_copied, 2, h, k - 1, 2 if proj else 0)
                    for j in range(NT):
                        last = product(j_bank[0][:], [t[:, w % 2, 1, j * P:(j + 1) * P] for t in kv],
                                       [t[:, j, :] for t in probT], j == 0, j == NT - 1)
                    last.then_inc(pv_mm, 1)

                def project_out(i):
                    if not value:
                        return
                    w = k - 2
                    if i == 0:
                        need(pe, o_lo, 1, h, w, 1)
                        wait(pe, wo_lo, h + (1 if k >= 2 else 0))
                    need(pe, w_added, 4, h, w, i - 1)
                    product(w_bank[i % 2][:], [t[:, i * P:(i + 1) * P] for t in oT],
                            [t[:] for t in wo]).then_inc(w_mm, 1)

                def key_value(half):
                    if not proj:
                        return
                    if half == 0:
                        wait(pe, wkv_lo, h + 1)
                        need(pe, q_lo, 1, h, k - 1, 1)
                        need(pe, q_squared, 1, h, k - 1, 1)
                    else:
                        need(pe, kv_copied, 2, h, k - 1, 2)
                        if value:
                            need(pe, o_lo, 1, h, k - 2, 1)
                    for a in range(2):
                        t0 = (2 * half + a) * P
                        for cj in range(CT):
                            last = product(j_bank[1 - half][:, a * 2 * HD:(a + 1) * 2 * HD],
                                           [t[:, k, cj, t0:t0 + P] for t in cT],
                                           [t[:, cj, :] for t in wkv], cj == 0, cj == CT - 1)
                    last.then_inc(kv_mm, 1)

                def query():
                    if not proj:
                        return
                    wait(pe, wq_lo, h + 1)
                    need(pe, kv_copied, 2, h, k, 1)
                    if isinstance(h, int) and h == 0:
                        pe.wait_ge(turned_lo, TURN["F", k] + 4)
                    for dj in range(DT):
                        last = product(j_bank[1][:], [t[:, dj * HD:(dj + 1) * HD] for t in wq],
                                       [t[:, k, dj, :] for t in xnT], dj == 0, dj == DT - 1)
                    last.then_inc(q_mm, 1)

                def key_turn():
                    if not proj:
                        return
                    need(pe, k_scaled, 1, h, k, 1)
                    if score:
                        need(pe, p_lo, 4, h, k - 1, 3)
                    else:
                        pe.wait_ge(turned_lo, TURNS)
                    for j in range(NT):
                        last = pe.transpose(t_bank[0][:, j * P:(j + 1) * P], kv_raw[:, j, 0:HD], ident[:])
                    last.then_inc(kT_mm, 1)

                def query_squares():
                    if not proj:
                        return
                    need(pe, q_squared, 1, h, k, 1)
                    if score:
                        need(pe, p_lo, 4, h, k - 1, 2)
                    for i in range(NT):
                        last = pe.matmul(t_bank[1][:, i:i + 1], sq[:, i * P:(i + 1) * P], ones[:], start=True,
                                         stop=True)
                    last.then_inc(q_ss_mm, 1)

                scores(0)
                scores(1)
                values()
                key_value(0)
                probs(0)
                scores(2)
                key_value(1)
                probs(1)
                scores(3)
                project_out(0)
                query()
                probs(2)
                project_out(1)
                key_turn()
                project_out(2)
                query_squares()
                probs(3)
                project_out(3)

            pe.wait_ge(const_ready, 2)
            step(0, 0, score=False, value=False)
            step(0, 1, value=False)
            step(0, 2)
            step(0, 3)
            with pe.Fori(1, H) as h:
                for k in range(B):
                    step(h, k)
            step(H, 0, proj=False)
            step(H, 1, proj=False, score=False)

            for i in range(NT):
                turn(TURNS + i, xn[:, i, :], xn_ready, XNS + i + 1)

            def expert_step(it, k, up=True, down=True):
                def gate_up(j):
                    if not up:
                        return
                    bank = (3 * k + j) % 2
                    if j == 0:
                        need_e(pe, gu_lo, 1, it, k, 1)
                    need_e(pe, silu_ready, IT, it, k, j - 1)
                    for dj in range(DT):
                        last = product(s_bank[bank][0:IW[j], :], [cols(a, 0, dj, j) for a in gu_w[k % 2]],
                                       [t[:, 0, dj, :] for t in xnT], dj == 0, dj == DT - 1)
                    last.then_inc(g_mm, 1)
                    need_e(pe, h_ready, IT, it, k, j - 1)
                    for dj in range(DT):
                        last = product(t_bank[bank][0:IW[j], :], [cols(a, 1, dj, j) for a in gu_w[k % 2]],
                                       [t[:, 0, dj, :] for t in xnT], dj == 0, dj == DT - 1)
                    last.then_inc(u_mm, 1)

                def project_down(t):
                    if not down:
                        return
                    e = k - 1
                    if t == 0:
                        need_e(pe, h_hi, IT, it, e, IT)
                        need_e(pe, h_lo, IT, it, e, IT)
                        need_e(pe, dn_lo, 1, it, e, 1)
                    need_e(pe, y_added, NT, it, e, t - 1)
                    for j in range(IT):
                        last = product(w_bank[t % 2][:], [a[0:IW[j], j, t * P:(t + 1) * P] for a in hT[e % 2]],
                                       [a[0:IW[j], j * D:(j + 1) * D] for a in dn_w[e % 2]], j == 0, j == IT - 1)
                    last.then_inc(d_mm, 1)

                gate_up(0)
                project_down(0)
                project_down(1)
                gate_up(1)
                project_down(2)
                gate_up(2)
                project_down(3)

            pe.wait_ge(turned_lo, TURNS + NT)
            expert_step(0, 0, down=False)
            expert_step(0, 1)
            with pe.Fori(1, E // 2) as it:
                expert_step(it, 0)
                expert_step(it, 1)
            expert_step(E // 2, 0, up=False)

        @block.scalar
        def _(act):
            def copy_hi(dst, src):
                return nc.scalar.copy(dst, src)

            def turned_tile(kind, b, i, n):
                act.wait_ge(turned, n + 1)
                dst = probT[0][:, :, i * P:(i + 1) * P] if kind == "P" else xnT[0][:, b, :, i * P:(i + 1) * P]
                copy_hi(dst, t_bank[n % 2][:].rearrange("p (j q) -> p j q", j=4)).then_inc(turned_hi, 1)

            act.wait_ge(vec_in, 16)
            nc.scalar.activation(tanh_g[:], vec[:, G_X:G_X + 4], ACT.Tanh).then_inc(gates_tanh, 1)
            nc.scalar.activation(small[:, 0:NBITS], vec[:, MASK:MASK + NBITS], ACT.Tanh, scale=0.5).then_inc(
                mask_tanh, 1)
            for kind, b in L0_ORDER:
                if kind == "K":
                    act.wait_ge(chunk_in[b % 2], 16 * (b // 2 + 1))
                    at = 2 * (b % 2)
                    if b == 0:
                        copy_hi(w0s[0][:], stage[:, at, :]).then_inc(chunk_hi, 1)
                    else:
                        copy_hi(cT[0][:, b - 1, :, :], stage[:, at:at + 2, :]).then_inc(chunk_hi, 1)
                elif kind in "ADF":
                    for i in range(NT):
                        turned_tile(kind, b, i, TURN[kind, b] + i)
                elif kind == "Q":
                    for n, bias in enumerate((BQ, BK)):
                        act.wait_ge(qk0_mm, 2 * b + n + 1)
                        wait(act, e0_mm, 4 * b)
                        nc.scalar.activation(qT[0][:, n, :], j_bank[n][:], ACT.Identity,
                                             bias=vec[:, bias:bias + 1]).then_inc(qk0_hi, 1)
                elif kind == "S":
                    for i in range(NT):
                        n = PROB[kind, b] + i
                        act.wait_ge(e0_max, n + 1)
                        if b:
                            act.wait_ge(turned, TURN["P", b - 1] + i + 1)
                        nc.scalar.activation(prob[:, i, :], s_bank[i % 2][:], ACT.Exp, bias=neg_max[:, b % 2, i:i + 1],
                                             accum_out=row_sum[:, b % 2, i:i + 1]).then_inc(e0_exp, 1)
                elif kind == "P":
                    for i in range(NT):
                        turned_tile(kind, b, i, TURN[kind, b] + i)
                elif kind == "G":
                    r = NSPLIT + b
                    act.wait_ge(chunk_in[r % 2], 16 * (r // 2 + 1))
                    at = 2 * (r % 2)
                    if b < DT * NBITS:
                        nc.scalar.activation(stage[:, at:at + 2, :], stage[:, at:at + 2, :], ACT.Tanh,
                                             scale=0.5).then_inc(bit_tanh, 1)
                        if b % NBITS == NBITS - 1:
                            act.wait_ge(bit_added, b + 1)
                            copy_hi(wf[0][:, b // NBITS, :], bit_acc).then_inc(wf_hi, 1)

            def step(h, k, proj=True, score=True, value=True):
                def softmax(i):
                    if not score:
                        return
                    u = k - 1
                    need(act, s_max, 4, h, u, i + 1)
                    need(act, p_turned, 4, h, u - 1, i + 1)
                    nc.scalar.activation(prob[:, i, :], s_bank[i % 2][:], ACT.Exp,
                                         bias=neg_bias[:, u % 2, i:i + 1], scale=q_scale[:, u % 2, i:i + 1],
                                         accum_out=row_sum[:, u % 2, i:i + 1]).then_inc(p_exp, 1)

                def probs_hi(i):
                    if not score:
                        return
                    need(act, p_turned, 4, h, k - 1, i + 1)
                    copy_hi(probT[0][:, :, i * P:(i + 1) * P],
                            t_bank[i % 2][:].rearrange("p (j q) -> p j q", j=4)).then_inc(p_hi, 1)

                def key_value_rows(half):
                    if not proj:
                        return
                    need(act, kv_mm, 2, h, k, half + 1)
                    if half == 0:
                        need(act, kT_mm, 1, h, k - 1, 1)
                        need(act, v_lo, 1, h, k - 1, 1)
                    nc.scalar.copy(kv_raw[:, 2 * half:2 * half + 2, :],
                                   j_bank[1 - half][:].rearrange("p (a c) -> p a c", a=2)).then_inc(kv_copied, 1)

                if k == 0 and proj:
                    wait(act, wkv_in, h * 16 + 16)
                    need(act, kv_mm, 2, h, -1, 2)
                    copy_hi(wkv[0][:, :, :].rearrange("p a c -> p (a c)"), stage[:, 0, :]).then_inc(wkv_hi, 1)
                if k == 2:
                    wait(act, wo_in, h * 16 + 16)
                    need(act, w_mm, 4, h, -1, 4)
                    copy_hi(wo[0][:], stage[:, 2, :]).then_inc(wo_hi, 1)
                softmax(0)
                if k == 0 and proj:
                    wait(act, wq_in, h * 16 + 16)
                    need(act, q_mm, 1, h, -1, 1)
                    copy_hi(wq[0][:], stage[:, 1, :]).then_inc(wq_hi, 1)
                softmax(1)
                if value:
                    need(act, pv_mm, 1, h, k - 2, 1)
                    need(act, w_mm, 4, h, k - 3, 4)
                    copy_hi(oT[0][:], j_bank[0][:]).then_inc(o_hi, 1)
                key_value_rows(0)
                probs_hi(0)
                softmax(2)
                key_value_rows(1)
                if proj:
                    need(act, kv_copied, 2, h, k, 2)
                    need(act, k_scaled, 1, h, k - 1, 1)
                    for i in range(NT):
                        nc.scalar.activation(ksq[:, i, :], kv_raw[:, i, 0:HD], ACT.Square, scale=HD ** -0.5,
                                             accum_out=k_ss[:, i:i + 1]).then_inc(k_squares, 1)
                probs_hi(1)
                softmax(3)
                if proj:
                    need(act, q_mm, 1, h, k, 1)
                    need(act, s_mm, 4, h, k - 2, 4)
                    copy_hi(qT[0][:, k % 2, :], j_bank[1][:]).then_inc(q_hi, 1)
                    need(act, q_ss_mm, 1, h, k - 1, 1)
                    nc.scalar.activation(sq[:], j_bank[1][:], ACT.Square).then_inc(q_squared, 1)
                probs_hi(2)
                if proj:
                    need(act, kT_mm, 1, h, k, 1)
                    need(act, s_mm, 4, h, k - 2, 4)
                    nc.scalar.activation(kv[0][:, k % 2, 0, :], t_bank[0][:], ACT.Copy,
                                         scale=gain[:]).then_inc(kT_hi, 1)
                probs_hi(3)

            act.wait_ge(gain_ready, 1)
            step(0, 0, score=False, value=False)
            step(0, 1, value=False)
            step(0, 2)
            step(0, 3)
            with act.Fori(1, H) as h:
                for k in range(B):
                    step(h, k)
            step(H, 0, proj=False)
            step(H, 1, proj=False, score=False)

            for i in range(NT):
                turned_tile("M", 0, i, TURNS + i)

            def gate_up_hi(it, k):
                need_e(act, gu_in, 16, it, k, 16)
                need_e(act, u_mm, IT, it, k - 2, IT)
                copy_hi(gu_w[k % 2][0], gu_stage).then_inc(gu_hi, 1)

            def expert_step(it, k, more=True):
                def silu(j):
                    need_e(act, g_mm, IT, it, k, j + 1)
                    need_e(act, h_ready, IT, it, k, j - 1)
                    g = (IT * k + j) % 2
                    nc.scalar.activation(prob[0:IW[j], g, :], s_bank[g][0:IW[j], :], ACT.Silu).then_inc(silu_ready, 1)

                def inner_hi(j):
                    need_e(act, h_ready, IT, it, k, j + 1)
                    if j == 0:
                        need_e(act, d_mm, NT, it, k - 2, NT)
                    copy_hi(hT[k % 2][0][0:IW[j], j, :],
                            prob[0:IW[j], 2 + (IT * k + j) % 2, :]).then_inc(h_hi, 1)

                silu(0)
                need_e(act, dn_in, 16, it, k, 16)
                need_e(act, d_mm, NT, it, k - 2, NT)
                copy_hi(dn_w[k % 2][0], dn_stage).then_inc(dn_hi, 1)
                inner_hi(0)
                silu(1)
                if more:
                    gate_up_hi(it, k + 1)
                inner_hi(1)
                silu(2)
                inner_hi(2)

            act.wait_ge(q_mm, B * H)
            act.wait_ge(kv_mm, 2 * B * H)
            gate_up_hi(0, 0)
            expert_step(0, 0)
            expert_step(0, 1)
            with act.Fori(1, E // 2 - 1) as it:
                expert_step(it, 0)
                expert_step(it, 1)
            expert_step(E // 2 - 1, 0)
            expert_step(E // 2 - 1, 1, more=False)

        @block.vector
        def _(dve):
            done, tiles_seen = [0], [0]

            def then_wait(ins):
                done[0] += 1
                ins.then_inc(dve_own, 1)
                dve.wait_ge(dve_own, done[0])

            def lower(dst, src, hi):
                return nc.vector.tensor_tensor(dst, src, hi, ALU.subtract)

            def tile_moments(b, i):
                n = tiles_seen[0]
                tiles_seen[0] += 1
                wait(dve, moments, n - 3)
                then_wait(nc.vector.bn_stats(stats[:, n % 4, :], x_sb[:, b, i, :]))
                nc.vector.bn_aggr(mean_var[:, b, i, :], stats[:, n % 4, :]).then_inc(moments, 1)

            def turned_tile(kind, b, i, n):
                dve.wait_ge(turned_hi, n + 1)
                where = [t[:, :, i * P:(i + 1) * P] if kind == "P" else t[:, b, :, i * P:(i + 1) * P]
                         for t in (probT if kind == "P" else xnT)]
                lower(where[1], t_bank[n % 2][:].rearrange("p (j q) -> p j q", j=4), f32(where[0])).then_inc(
                    turned_lo, 1)

            nc.vector.memset(ones[:], 1.0).then_inc(const_ready, 1)
            nc.vector.memset(minus_half[:], -0.5).then_inc(const_ready, 1)
            nc.vector.memset(eps[:], EPS).then_inc(const_ready, 1)
            dve.wait_ge(vec_in, 16)
            nc.vector.tensor_tensor(gain[:], vec[:, GQ:GQ + 1], vec[:, GK:GK + 1], ALU.mult).then_inc(gain_ready, 1)
            dve.wait_ge(gates_tanh, 1)
            dve.wait_ge(mask_tanh, 1)
            then_wait(nc.vector.tensor_scalar(small[:, 4:8], small[:, 0:4], 0.5, 0.5, ALU.mult, ALU.add))
            then_wait(nc.vector.tensor_tensor(small[:, 0:4], small[:, 4:8], vec[:, EXPS:EXPS + NBITS], ALU.mult))
            then_wait(nc.vector.tensor_scalar(small[:, 4:8], small[:, 0:4], vec[:, SCALE:SCALE + 1],
                                              tanh_g[:, 2:3], ALU.mult, ALU.mult))
            then_wait(nc.vector.tensor_scalar(bit_w[:], small[:, 4:8], 0.5, None, ALU.mult))

            dve.wait_ge(x_in[0], 16)
            for i in range(NT):
                tile_moments(0, i)
            for kind, b in L0_ORDER:
                if kind in "ADF":
                    for i in range(NT):
                        turned_tile(kind, b, i, TURN[kind, b] + i)
                    if kind == "A" and b + 1 < B:
                        dve.wait_ge(x_in[b + 1], 16)
                        for i in range(NT):
                            tile_moments(b + 1, i)
                elif kind == "Q":
                    for n, bias in enumerate((BQ, BK)):
                        dve.wait_ge(qk0_hi, 2 * b + n + 1)
                        nc.vector.scalar_tensor_tensor(
                            out=qT[1][:, n, :], in0=j_bank[n][:], scalar=vec[:, bias:bias + 1],
                            in1=f32(qT[0][:, n, :]), op0=ALU.add, op1=ALU.subtract).then_inc(qk0_lo, 1)
                elif kind == "S":
                    def scaled(i):
                        dve.wait_ge(e0_exp, PROB[kind, b] + i + 1)
                        then_wait(nc.vector.reciprocal(inv_sum[:, b % 2, i:i + 1], row_sum[:, b % 2, i:i + 1]))
                        nc.vector.tensor_scalar(prob[:, i, :], prob[:, i, :], inv_sum[:, b % 2, i:i + 1], None,
                                                ALU.mult).then_inc(e0_scaled, 1)
                    for i in range(NT):
                        dve.wait_ge(e0_mm, PROB[kind, b] + i + 1)
                        nc.vector.tensor_reduce(neg_max[:, b % 2, i:i + 1], s_bank[i % 2][:], AX_X, ALU.max,
                                                negate=True).then_inc(e0_max, 1)
                        if i:
                            scaled(i - 1)
                    scaled(NT - 1)
                elif kind == "P":
                    for i in range(NT):
                        turned_tile(kind, b, i, TURN[kind, b] + i)
                elif kind in "CE":
                    for i in range(NT):
                        n = WIDE[kind, b] + i
                        dve.wait_ge(wide_mm, n + 1)
                        here = x_sb[:, b, i, :]
                        if kind == "C":
                            nc.vector.scalar_tensor_tensor(
                                out=here, in0=w_bank[n % 2][:], scalar=tanh_g[:, 0:1], in1=here,
                                op0=ALU.mult, op1=ALU.add).then_inc(wide_added, 1)
                        else:
                            dve.wait_ge(bias_added, NT * b + i + 1)
                            nc.vector.tensor_tensor(here, w_bank[n % 2][:], here, ALU.add).then_inc(wide_added, 1)
                        dve.wait_ge(wide_added, n + 1)
                        tile_moments(b, i)
                elif kind == "G":
                    j, n = divmod(b, NBITS)
                    at = 2 * ((NSPLIT + b) % 2)
                    factor = bit_w[:, n:n + 1] if j < DT else vec[:, BEXPS + n:BEXPS + n + 1]
                    dve.wait_ge(bit_diff, b + 1)
                    if n == 0:
                        wait(dve, wf_lo, j)
                        nc.vector.tensor_scalar(bit_acc, stage[:, at, :], factor, None, ALU.mult).then_inc(
                            bit_added, 1)
                    else:
                        nc.vector.scalar_tensor_tensor(out=bit_acc, in0=stage[:, at, :], scalar=factor, in1=bit_acc,
                                                       op0=ALU.mult, op1=ALU.add).then_inc(bit_added, 1)
                    dve.wait_ge(bit_added, b + 1)
                    if b == NBIT_CHUNKS - 1:
                        steps = float(2 ** NBITS - 1)
                        then_wait(nc.vector.tensor_scalar(bias_t, bit_acc, -1.0, 1.0, ALU.max, ALU.min))
                        then_wait(nc.vector.tensor_scalar(bias_t, bias_t, steps, None, ALU.mult))
                        then_wait(nc.vector.tensor_scalar(bias_t, bias_t, ROUND, None, ALU.add))
                        then_wait(nc.vector.tensor_scalar(bias_t, bias_t, -ROUND, 1.0 / steps, ALU.add, ALU.mult))
                        nc.vector.tensor_scalar(bias_t, bias_t, vec[:, BSCALE:BSCALE + 1], tanh_g[:, 2:3],
                                                ALU.mult, ALU.mult).then_inc(bias_ready, 1)

            dve.wait_ge(idx_in, 32)
            then_wait(nc.vector.tensor_copy(idx_f[:], idx[:]))
            for e in range(E):
                then_wait(nc.vector.scalar_tensor_tensor(
                    out=picked[:], in0=idx_f[:], scalar=float(e), in1=topw[:], op0=ALU.is_equal, op1=ALU.mult))
                then_wait(nc.vector.tensor_reduce(share[:, :, e:e + 1], picked[:], AX_X, ALU.add))
            then_wait(nc.vector.tensor_scalar(share[:], share[:], tanh_g[:, 3:4], None, ALU.mult))

            own_max, own_inv = sem("own_max"), sem("own_inv")

            def step(h, k, proj=True, score=True, value=True):
                def maximum(i):
                    if not score:
                        return
                    u = k - 1
                    need(dve, s_mm, 4, h, u, i + 1)
                    nc.vector.tensor_reduce(neg_max[:, u % 2, i:i + 1], s_bank[i % 2][:], AX_X, ALU.max,
                                            negate=True).then_inc(own_max, 1)
                    if i == 0:
                        need(dve, q_scale_ready, 1, h, u, 1)
                    need(dve, own_max, 4, h, u, i + 1)
                    nc.vector.tensor_tensor(neg_bias[:, u % 2, i:i + 1], neg_max[:, u % 2, i:i + 1],
                                            q_scale[:, u % 2, i:i + 1], ALU.mult).then_inc(s_max, 1)

                def probs_lo(i):
                    if not score:
                        return
                    need(dve, p_hi, 4, h, k - 1, i + 1)
                    hi, lo = [t[:, :, i * P:(i + 1) * P] for t in probT]
                    lower(lo, t_bank[i % 2][:].rearrange("p (j q) -> p j q", j=4), f32(hi)).then_inc(p_lo, 1)

                def add(i):
                    if not value:
                        return
                    w = k - 2
                    need(dve, w_mm, 4, h, w, i + 1)
                    if i == 0:
                        need(dve, own_inv, 2, h, w, 2)
                    here = x_sb[:, w % B, i, :]
                    nc.vector.scalar_tensor_tensor(out=here, in0=w_bank[i % 2][:], scalar=inv_sum[:, w % 2, i:i + 1],
                                                   in1=here, op0=ALU.mult, op1=ALU.add).then_inc(w_added, 1)

                maximum(0)
                maximum(1)
                if value:
                    w = k - 2
                    nc.vector.reciprocal(inv_sum[:, w % 2, :], row_sum[:, w % 2, :]).then_inc(own_inv, 1)
                    need(dve, own_inv, 2, h, w, 1)
                    nc.vector.tensor_scalar(inv_sum[:, w % 2, :], inv_sum[:, w % 2, :], tanh_g[:, 1:2], None,
                                            ALU.mult).then_inc(own_inv, 1)
                    need(dve, o_hi, 1, h, w, 1)
                    lower(oT[1][:], j_bank[0][:], f32(oT[0][:])).then_inc(o_lo, 1)
                probs_lo(0)
                maximum(2)
                probs_lo(1)
                maximum(3)
                if proj:
                    need(dve, kv_copied, 2, h, k, 2)
                    need(dve, pv_mm, 1, h, k - 2, 1)
                    nc.vector.tensor_copy(kv[0][:, k % 2, 1, :].rearrange("p (j c) -> p j c", j=NT),
                                          kv_raw[:, :, HD:2 * HD]).then_inc(v_hi, 1)
                add(0)
                if proj:
                    need(dve, q_hi, 1, h, k, 1)
                    need(dve, q_squared, 1, h, k, 1)
                    lower(qT[1][:, k % 2, :], j_bank[1][:], f32(qT[0][:, k % 2, :])).then_inc(q_lo, 1)
                probs_lo(2)
                add(1)
                if proj:
                    need(dve, kT_hi, 1, h, k, 1)
                    nc.vector.scalar_tensor_tensor(
                        out=kv[1][:, k % 2, 0, :], in0=t_bank[0][:], scalar=gain[:], in1=f32(kv[0][:, k % 2, 0, :]),
                        op0=ALU.mult, op1=ALU.subtract).then_inc(kT_lo, 1)
                add(2)
                if proj:
                    need(dve, q_ss_mm, 1, h, k, 1)
                    nc.vector.tensor_scalar(q_ss[:, k % 2, :], t_bank[1][:, 0:NT], HD * EPS, None,
                                            ALU.add).then_inc(q_ss_out, 1)
                probs_lo(3)
                add(3)

            step(0, 0, score=False, value=False)
            step(0, 1, value=False)
            step(0, 2)
            step(0, 3)
            with dve.Fori(1, H) as h:
                for k in range(B):
                    step(h, k)
            dve.wait_ge(w_added, 4 * (B * (H - 1) + 1))
            for i in range(NT):
                tile_moments(0, i)
            step(H, 0, proj=False)
            step(H, 1, proj=False, score=False)
            for i in range(NT):
                turned_tile("M", 0, i, TURNS + i)

            def expert_step(it, k, up=True, down=True):
                def inner(j):
                    if not up:
                        return
                    g = (IT * k + j) % 2
                    need_e(dve, silu_ready, IT, it, k, j + 1)
                    need_e(dve, u_mm, IT, it, k, j + 1)
                    need_e(dve, h_lo, IT, it, k, j - 1)
                    nc.vector.tensor_tensor(prob[0:IW[j], 2 + g, :], t_bank[g][0:IW[j], :], prob[0:IW[j], g, :],
                                            ALU.mult).then_inc(h_ready, 1)

                def add(t):
                    if not down:
                        return
                    e = k - 1
                    need_e(dve, d_mm, NT, it, e, t + 1)
                    here = x_sb[:, 0, t, :]
                    at = it * 2 + e
                    factor = share[:, t, at:at + 1] if isinstance(at, int) else share[:, t, bass.ds(at, 1)]
                    nc.vector.scalar_tensor_tensor(out=here, in0=w_bank[t % 2][:], scalar=factor, in1=here,
                                                   op0=ALU.mult, op1=ALU.add).then_inc(y_added, 1)

                inner(0)
                add(0)
                add(1)
                inner(1)
                add(2)
                inner(2)
                add(3)

            expert_step(0, 0, down=False)
            expert_step(0, 1)
            with dve.Fori(1, E // 2) as it:
                expert_step(it, 0)
                expert_step(it, 1)
            expert_step(E // 2, 0, up=False)

        @block.gpsimd
        def _(pool):
            done = [0]

            def then_wait(ins):
                done[0] += 1
                ins.then_inc(pool_own, 1)
                pool.wait_ge(pool_own, done[0])

            def lower(dst, src, hi):
                return nc.gpsimd.tensor_tensor(dst, src, hi, ALU.subtract)

            def norm(b, seen, first):
                pool.wait_ge(moments, seen)
                then_wait(nc.gpsimd.tensor_scalar(var_eps[:], mean_var[:, b, :, 1], EPS, None, ALU.add))
                then_wait(nc.gpsimd.tensor_tensor(rstd[:], var_eps[:], minus_half[:], ALU.pow))
                for i in range(NT):
                    if first + i >= NT:
                        pool.wait_ge(turned, XN_TURN[first + i - NT] + 1)
                    nc.gpsimd.tensor_scalar(xn[:, i, :], x_sb[:, b, i, :], mean_var[:, b, i, 0:1], rstd[:, i:i + 1],
                                            ALU.subtract, ALU.mult).then_inc(xn_ready, 1)

            XN_TURN = {XN[key] + i: TURN[key] + i for key in XN for i in range(NT)}
            seen, order = {}, [("A", 0)]
            for key in L0_ORDER:
                if key[0] == "A" and key[1] + 1 < B:
                    order.append(("A", key[1] + 1))
                elif key[0] in "CE":
                    order.append(("D" if key[0] == "C" else "F", key[1]))
            for n, key in enumerate(order):
                seen[key] = NT * (n + 1)

            nc.gpsimd.memset(ident[:], 0.0).then_inc(ident_ready, 1)
            pool.wait_ge(ident_ready, 1)
            nc.gpsimd.affine_select(out=ident[:], in_=ident[:], compare_op=ALU.not_equal, fill=1.0, base=0,
                                    pattern=[[-1, P]], channel_multiplier=1).then_inc(ident_ready, 1)
            pool.wait_ge(const_ready, 3)
            for kind, b in L0_ORDER:
                if kind == "K":
                    pool.wait_ge(chunk_hi, b + 1)
                    at = 2 * (b % 2)
                    if b == 0:
                        lower(w0s[1][:], stage[:, at, :], f32(w0s[0][:])).then_inc(chunk_lo, 1)
                    else:
                        lower(cT[1][:, b - 1, :, :], stage[:, at:at + 2, :], f32(cT[0][:, b - 1, :, :])).then_inc(
                            chunk_lo, 1)
                elif kind in "ADF":
                    norm(b, seen[kind, b], XN[kind, b])
                elif kind == "B":
                    pool.wait_ge(bias_ready, 1)
                    pool.wait_ge(xn_ready, XN["D", b] + NT)
                    for i in range(NT):
                        nc.gpsimd.tensor_tensor(x_sb[:, b, i, :], x_sb[:, b, i, :], bias_t,
                                                ALU.add).then_inc(bias_added, 1)
                elif kind == "G":
                    r = NSPLIT + b
                    at = 2 * (r % 2)
                    if b < DT * NBITS:
                        pool.wait_ge(bit_tanh, b + 1)
                    else:
                        pool.wait_ge(chunk_in[r % 2], 16 * (r // 2 + 1))
                    nc.gpsimd.tensor_tensor(stage[:, at, :], stage[:, at, :], stage[:, at + 1, :],
                                            ALU.subtract).then_inc(bit_diff, 1)
                    if b < DT * NBITS and b % NBITS == NBITS - 1:
                        pool.wait_ge(wf_hi, b // NBITS + 1)
                        lower(wf[1][:, b // NBITS, :], bit_acc, f32(wf[0][:, b // NBITS, :])).then_inc(wf_lo, 1)

            def split_lo(dst, slot, h, hi_done, lo_done):
                hi, lo = dst
                wait(pool, hi_done, h + 1)
                lower(lo, stage[:, slot, :], f32(hi)).then_inc(lo_done, 1)

            k_own = sem("k_own")

            def step(h, k):
                if k == 0:
                    split_lo([t[:, :, :].rearrange("p a c -> p (a c)") for t in wkv], 0, h, wkv_hi, wkv_lo)
                    split_lo([t[:] for t in wq], 1, h, wq_hi, wq_lo)
                if k == 2:
                    split_lo([t[:] for t in wo], 2, h, wo_hi, wo_lo)
                need(pool, k_squares, 4, h, k, 4)
                nc.gpsimd.tensor_tensor(k_ms[:], k_ss[:], eps[:], ALU.add).then_inc(k_own, 1)
                need(pool, k_own, 2, h, k, 1)
                nc.gpsimd.tensor_tensor(k_rs[:], k_ms[:], minus_half[:], ALU.pow).then_inc(k_own, 1)
                need(pool, k_own, 2, h, k, 2)
                keys = kv_raw[:, :, 0:HD]
                nc.gpsimd.tensor_tensor(keys, keys, k_rs[:].unsqueeze(2).to_broadcast([P, NT, HD]),
                                        ALU.mult).then_inc(k_scaled, 1)
                hi, lo = [t[:, k % 2, 1, :].rearrange("p (j c) -> p j c", j=NT) for t in kv]
                need(pool, v_hi, 1, h, k, 1)
                lower(lo, kv_raw[:, :, HD:2 * HD], f32(hi)).then_inc(v_lo, 1)
                need(pool, q_ss_out, 1, h, k, 1)
                nc.gpsimd.tensor_tensor(q_scale[:, k % 2, :], q_ss[:, k % 2, :], minus_half[:],
                                        ALU.pow).then_inc(q_scale_ready, 1)

            for k in range(B):
                step(0, k)
            with pool.Fori(1, H) as h:
                for k in range(B):
                    step(h, k)

            XN_TURN.update({XNS + i: TURNS + i for i in range(NT)})
            norm(0, NT * len(order) + NT, XNS)

            def gate_up_lo(it, k):
                need_e(pool, gu_hi, 1, it, k, 1)
                lower(gu_w[k % 2][1], gu_stage, f32(gu_w[k % 2][0])).then_inc(gu_lo, 1)

            def expert_step(it, k, more=True):
                def inner_lo(j):
                    need_e(pool, h_hi, IT, it, k, j + 1)
                    lower(hT[k % 2][1][0:IW[j], j, :], prob[0:IW[j], 2 + (IT * k + j) % 2, :],
                          f32(hT[k % 2][0][0:IW[j], j, :])).then_inc(h_lo, 1)

                need_e(pool, dn_hi, 1, it, k, 1)
                lower(dn_w[k % 2][1], dn_stage, f32(dn_w[k % 2][0])).then_inc(dn_lo, 1)
                inner_lo(0)
                if more:
                    gate_up_lo(it, k + 1)
                inner_lo(1)
                inner_lo(2)

            gate_up_lo(0, 0)
            expert_step(0, 0)
            expert_step(0, 1)
            with pool.Fori(1, E // 2 - 1) as it:
                expert_step(it, 0)
                expert_step(it, 1)
            expert_step(E // 2 - 1, 0)
            expert_step(E // 2 - 1, 1, more=False)


def kernel(**inputs):
    import numpy as np
    import concourse.bacc as bacc
    from concourse.bass_utils import run_bass_kernel_spmd

    a = {name: np.asarray(value) for name, value in inputs.items()}

    def whole(v):
        return np.ascontiguousarray(v)

    ctxT = a["ctx_1024"].transpose(0, 2, 1).reshape(B, CT, P, S)
    columns = [a["L0_xattn_bq"], a["L0_xattn_bk"], a["L1_xattn_gq"], a["L1_xattn_gk"]]
    for name in ("g_xattn", "g_ffn", "L0_ffn_exps", "L0_ffn_bexps", "L0_ffn_mask_weight", "L0_ffn_scale",
                 "L0_ffn_biasscale"):
        columns += [np.broadcast_to(v, (P,)) for v in a[name]]
    vecs = np.stack(columns, axis=1)
    w0 = np.stack([a[n].T.reshape(CT, P, P).transpose(1, 0, 2) for n in ("L0_xattn_Wq", "L0_xattn_Wk")], axis=1)
    planes = np.stack([a[n].transpose(2, 1, 0).reshape(NBITS, DT, P, D) for n in ("L0_ffn_pweight", "L0_ffn_nweight")],
                      axis=2).transpose(1, 0, 2, 3, 4)
    bias = np.stack([np.broadcast_to(a[n].T[:, None, :], (NBITS, P, D)) for n in ("L0_ffn_pbias", "L0_ffn_nbias")],
                    axis=1)
    bits = np.concatenate([planes.reshape(DT * NBITS, 2, P, D), bias], axis=0)
    wk, wv = (a[n].reshape(CT, P, H, HD).transpose(2, 1, 0, 3) for n in ("L1_xattn_Wk", "L1_xattn_Wv"))
    wkv = np.stack([wk, wv], axis=3).reshape(H, P, CT * 2 * HD)
    wq = a["L1_xattn_Wq"].reshape(DT, P, H, HD).transpose(2, 1, 0, 3).reshape(H, P, DT * HD)
    w1 = np.stack([wkv, wq, a["L1_xattn_Wo"].reshape(H, HD, D)], axis=0)
    w_gu = np.stack([a[n].transpose(0, 2, 1).reshape(E, DT, P, I).transpose(0, 2, 1, 3)
                     for n in ("L1_ffn_gate_weight", "L1_ffn_up_weight")], axis=2).reshape(E, P, 2 * DT * I)
    down = np.zeros((E, IT * P, D), a["L1_ffn_down_weight"].dtype)
    down[:, :I] = a["L1_ffn_down_weight"].transpose(0, 2, 1)
    w_dn = down.reshape(E, IT, P, D).transpose(0, 2, 1, 3).reshape(E, P, IT * D)

    def by_tile(v):
        return v.reshape(NT, P, TOPK).transpose(1, 0, 2)

    arrays = {
        "x": a["x"].reshape(B * S, D), "ctxT": ctxT, "vecs": vecs, "w0": w0.reshape(P, 2 * CT * P), "bits": bits,
        "w1": w1, "w_gu": w_gu, "w_dn": w_dn, "topk_idx": by_tile(a["L1_ffn_topk_idx"]),
        "topk_w": by_tile(a["L1_ffn_topk_weight"]),
    }
    arrays = {name: whole(v) for name, v in arrays.items()}
    nc = bacc.Bacc("TRN2", target_bir_lowering=False, num_devices=1, dynamic_dma_scratch_size=4096)
    args = [nc.dram_tensor(name, v.shape, mybir.dt.from_np(v.dtype), kind="ExternalInput").ap()
            for name, v in arrays.items()]
    out = nc.dram_tensor("out", (B * S, D), F32, kind="ExternalOutput").ap()
    flamingo_kernel(nc, *args, out)
    result = run_bass_kernel_spmd(nc, [arrays], core_ids=[0])
    return result.results[0]["out"].reshape(B, S, D)
```

```python
from contextlib import ExitStack

import concourse.bass as bass
from concourse import mybir

F32 = mybir.dt.float32
F32R = mybir.dt.float32r
I32 = mybir.dt.int32
ALU = mybir.AluOpType
ACT = mybir.ActivationFunctionType
AX_X = mybir.AxisListType.X

P = 128
B, S, D, C = 4, 512, 512, 256
NT = S // P
DT = D // P
CT = C // P
H, HD = 16, 128
NBITS = 4
E, I, TOPK = 16, 352, 4
IT = -(-I // P)
IW = [min(P, I - P * j) for j in range(IT)]
EPS = 1e-5
ROUND = 1.5 * 2.0 ** 23

BQ, BK, GQ, GK = range(4)
G_X, G_F, EXPS, BEXPS, MASK, SCALE, BSCALE = 4, 6, 8, 12, 16, 20, 21
NVEC = 22

L0_ORDER = [(word[0], int(word[1:])) for word in """
    K0 K1 Q0 K2 S0 m0 a0 A0 K3 K4 P0 m1 G0 G1 C0 G2 Q1 S1 G3 a1 A1 P1 G4 G5 d0 D0 G6 m2 C1 G7 G8 G9 Q2 S2 G10 a2 A2
    P2 G11 G12 d1 D1 G13 m3 C2 G14 G15 G16 G17 G18 G19 B0 B1 E0 Q3 S3 a3 A3 E1 f0 F0 d2 D2 P3 B2 C3 E2 f1 F1 d3 D3
    B3 f2 F2 E3 f3 F3""".split()]
NBIT_CHUNKS = (DT + 1) * NBITS


def numbered(kinds):
    found, n = {}, 0
    for key in L0_ORDER:
        if key[0] in kinds:
            found[key] = n
            n += 4
    return found, n


TURN, TURNS = numbered("ADFP")
XN, XNS = numbered("adf")
MOMENTS, NMOMENTS = numbered("mCE")
WIDE, WIDES = numbered("CE")
PROB, PROBS = numbered("S")
P_BANK = (1, 0, 1, 1)


def flamingo_kernel(nc, x, ctxT, vecs, w0, bits, w1, w_gu, w_dn, topk_idx, topk_w, out):
    x_tiles = x.rearrange("(b i p) d -> b p i d", b=B, p=P)
    out_tiles = out.rearrange("(b i p) d -> b p i d", b=B, p=P)

    with ExitStack() as ctx:
        def sb(name, shape, dt=F32):
            return ctx.enter_context(nc.sbuf_tensor(name, shape, dt))

        def sem(name):
            return ctx.enter_context(nc.semaphore(name))

        def hi_lo(name, shape):
            return [sb(f"{name}_{part}", shape, F32R) for part in ("hi", "lo")]

        def f32(ap):
            return ap.bitcast(F32)

        x_sb = sb("x_sb", [P, B, NT, D])
        xnT = hi_lo("xnT", [P, B, DT, S])
        cT = hi_lo("cT", [P, B, CT, S])
        probT = hi_lo("probT", [P, NT, S])
        kv = hi_lo("kv", [P, 2, 2, S])
        qT = hi_lo("qT", [P, 2, S])
        oT = hi_lo("oT", [P, S])
        wq = hi_lo("wq", [P, DT * HD])
        wkv = hi_lo("wkv", [P, CT, 2 * HD])
        wo = hi_lo("wo", [P, D])
        prob = sb("prob", [P, NT, S])
        xn = sb("xn", [P, NT, D])
        stage = sb("stage", [P, 4, S])
        kv_raw = sb("kv_raw", [P, NT, 2 * HD])
        sqs = hi_lo("sqs", [P, S])
        ident = sb("ident", [P, P])
        vec = sb("vec", [P, NVEC])
        ones = sb("ones", [P, 2], F32R)
        minus_half = sb("minus_half", [P, NT])
        eps = sb("eps", [P, NT])
        tanh_g = sb("tanh_g", [P, 4])
        small = sb("small", [P, 16])
        bit_w = sb("bit_w", [P, NBITS])
        gain = sb("gain", [P, 1])
        stats = sb("stats", [P, 4, 6])
        mean_var = sb("mean_var", [P, B, NT, 2])
        var_eps = sb("var_eps", [P, NT])
        rstd = sb("rstd", [P, B, NT])
        neg_max = sb("neg_max", [P, 2, NT])
        neg_bias = sb("neg_bias", [P, 2, NT])
        row_sum = sb("row_sum", [P, 2, NT])
        inv_sum = sb("inv_sum", [P, 2, NT])
        q_ss = sb("q_ss", [P, 2, NT])
        q_scale = sb("q_scale", [P, 2, NT])
        k_ss = sb("k_ss", [P, NT])
        k_ms = sb("k_ms", [P, NT])
        k_rs = sb("k_rs", [P, NT])
        idx = sb("idx", [P, NT, TOPK], I32)
        idx_f = sb("idx_f", [P, NT, TOPK])
        topw = sb("topw", [P, NT, TOPK])
        picked = sb("picked", [P, NT, TOPK])
        share = sb("share", [P, NT, E])

        sq = xn[:, 0, :]
        ksq = xn[:, 1, :].rearrange("p (i c) -> p i c", i=NT)
        bias_t = kv_raw[:, 0:2, :].rearrange("p a c -> p (a c)")
        bit_acc = kv_raw[:, 2:4, :].rearrange("p a c -> p (a c)")
        w0s = oT
        split_stage = [bias_t, stage[:, 0:2, :], stage[:, 2:4, :], x_sb[:, B - 1, 0:2, :], x_sb[:, B - 1, 2:4, :]]
        wf = [t[:, :, :, :].rearrange("p a b c -> p (a b) c") for t in kv]

        s_bank = [ctx.enter_context(nc.psum_tensor(f"s_bank{i}", [P, 512], F32)) for i in range(2)]
        t_bank = [ctx.enter_context(nc.psum_tensor(f"t_bank{i}", [P, 512], F32)) for i in range(2)]
        w_bank = [ctx.enter_context(nc.psum_tensor(f"w_bank{i}", [P, 512], F32)) for i in range(2)]
        j_bank = [ctx.enter_context(nc.psum_tensor(f"j_bank{i}", [P, 512], F32)) for i in range(2)]

        vec_in, idx_in = sem("vec_in"), sem("idx_in")
        x_in = [sem(f"x_in{b}") for b in range(B)]
        split_in = [sem(f"split_in{i}") for i in range(1 + B)]
        planes_in = [sem(f"planes_in{i}") for i in range(2)]
        wq_in, wkv_in, wo_in = sem("wq_in"), sem("wkv_in"), sem("wo_in")
        gu_in, dn_in, stored = sem("gu_in"), sem("dn_in"), sem("stored")
        ident_ready, const_ready, gain_ready = sem("ident_ready"), sem("const_ready"), sem("gain_ready")
        gates_tanh, mask_tanh, bit_w_ready, share_ready = (
            sem("gates_tanh"), sem("mask_tanh"), sem("bit_w_ready"), sem("share_ready"))
        dve_own, pool_own = sem("dve_own"), sem("pool_own")
        split_hi, split_lo = sem("split_hi"), sem("split_lo")
        bit_tanh, bit_diff, bit_added = sem("bit_tanh"), sem("bit_diff"), sem("bit_added")
        wf_hi, wf_lo, bias_ready = sem("wf_hi"), sem("wf_lo"), sem("bias_ready")
        moments, var_ready, rstd_ready, xn_ready, turned, turned_hi, turned_lo = (
            sem("moments"), sem("var_ready"), sem("rstd_ready"), sem("xn_ready"), sem("turned"), sem("turned_hi"), sem("turned_lo"))
        qk0_mm, qk0_hi, qk0_lo, e0_mm, e0_max, e0_exp, e0_inv, e0_scaled = (
            sem("qk0_mm"), sem("qk0_hi"), sem("qk0_lo"), sem("e0_mm"), sem("e0_max"), sem("e0_exp"), sem("e0_inv"),
            sem("e0_scaled"))
        wide_mm, wide_added, bias_added = sem("wide_mm"), sem("wide_added"), sem("bias_added")
        wq_hi, wq_lo, wkv_hi, wkv_lo, wo_hi, wo_lo = (
            sem("wq_hi"), sem("wq_lo"), sem("wkv_hi"), sem("wkv_lo"), sem("wo_hi"), sem("wo_lo"))
        kv_mm, kv_copied, k_squares, k_scaled, v_hi, v_lo = (
            sem("kv_mm"), sem("kv_copied"), sem("k_squares"), sem("k_scaled"), sem("v_hi"), sem("v_lo"))
        kT_mm, kT_hi, kT_lo = sem("kT_mm"), sem("kT_hi"), sem("kT_lo")
        q_mm, q_hi, q_lo, q_squared, sq_lo, q_ss_mm, q_ss_out, q_scale_ready = (
            sem("q_mm"), sem("q_hi"), sem("q_lo"), sem("q_squared"), sem("sq_lo"), sem("q_ss_mm"), sem("q_ss_out"),
            sem("q_scale_ready"))
        s_mm, s_max, p_exp, p_turned, p_hi, p_lo = (
            sem("s_mm"), sem("s_max"), sem("p_exp"), sem("p_turned"), sem("p_hi"), sem("p_lo"))
        pv_mm, o_hi, o_lo, w_mm, w_added = sem("pv_mm"), sem("o_hi"), sem("o_lo"), sem("w_mm"), sem("w_added")
        gu_hi, gu_lo, dn_hi, dn_lo = sem("gu_hi"), sem("gu_lo"), sem("dn_hi"), sem("dn_lo")
        g_mm, u_mm, silu_ready, h_ready, h_hi, h_lo, d_mm, y_added = (
            sem("g_mm"), sem("u_mm"), sem("silu_ready"), sem("h_ready"), sem("h_hi"), sem("h_lo"), sem("d_mm"),
            sem("y_added"))

        def wait(eng, s, value):
            if isinstance(value, int) and value <= 0:
                return
            eng.wait_ge(s, value)

        def need(eng, s, per, h, k, c):
            wait(eng, s, h * (B * per) + (per * k + c))

        def need_e(eng, s, per, it, k, c):
            wait(eng, s, it * (2 * per) + (per * k + c))

        GU = 2 * DT * I
        DN = IT * D
        w_area = [t[:, 1:B, :, :].rearrange("p b j s -> p (b j s)") for t in xnT]
        c_area = [t[:, :, :, :].rearrange("p b j s -> p (b j s)") for t in cT]
        gu_w = [[w_area[part][:, slot * GU:(slot + 1) * GU] for part in range(2)] for slot in range(2)]
        dn_w = [[c_area[part][:, slot * DN:(slot + 1) * DN] for part in range(2)] for slot in range(2)]
        x_area = x_sb[:, 1:B, :, :].rearrange("p b i d -> p (b i d)")
        gu_stage, dn_stage = x_area[:, 0:GU], x_area[:, GU:GU + DN]
        hT = [[t[:, 0:IT, :] for t in probT],
              [t[:, :, :, :].rearrange("p a b s -> p (a b) s")[:, 0:IT, :] for t in kv]]

        def cols(area, which, dj, j):
            at = (which * DT + dj) * I + j * P
            return area[:, at:at + IW[j]]

        block = ctx.enter_context(nc.Block())

        @block.sync
        def _(sp):
            def context(b):
                sp.dma_start(split_stage[1 + b], ctxT[b].rearrange("j p s -> p j s")).then_inc(split_in[1 + b], 16)

            def rows(b):
                sp.dma_start(x_sb[:, b, :, :], x_tiles[b]).then_inc(x_in[b], 16)

            def planes(g):
                if g < 2:
                    sp.wait_ge(split_lo, 2 + g)
                else:
                    sp.wait_ge(bit_added, g - 1)
                at = 2 * (g % 2)
                sp.dma_start(stage[:, at:at + 2, :], bits[g].rearrange("w p s -> p w s")).then_inc(
                    planes_in[g % 2], 16)

            sp.dma_start(split_stage[0], w0).then_inc(split_in[0], 16)
            context(0)
            sp.dma_start(vec[:], vecs).then_inc(vec_in, 16)
            rows(0)
            for b in range(1, B):
                context(b)
            rows(1)
            for g in range(NBIT_CHUNKS):
                planes(g)
                if g == 1:
                    rows(2)
                if g == 3:
                    sp.wait_ge(split_lo, 1 + B)
                    rows(3)
            sp.dma_start(idx[:], topk_idx).then_inc(idx_in, 16)
            sp.dma_start(topw[:], topk_w).then_inc(idx_in, 16)

            def head_weights(h):
                for n, (arrived, used) in enumerate(((wkv_in, wkv_lo), (wq_in, wq_lo), (wo_in, wo_lo))):
                    wait(sp, used, h)
                    src = w1[n, h] if isinstance(h, int) else w1[n, bass.ds(h, 1), :, :].rearrange("a p s -> p (a s)")
                    sp.dma_start(stage[:, n, :], src).then_inc(arrived, 16)

            sp.wait_ge(bit_added, NBIT_CHUNKS)
            head_weights(0)
            with sp.Fori(1, H) as h:
                head_weights(h)

            for b in range(1, B):
                sp.wait_ge(w_added, 4 * (B * (H - 1) + b + 1))
                sp.dma_start(out_tiles[b], x_sb[:, b, :, :]).then_inc(stored, 16)
            sp.wait_ge(stored, 16 * (B - 1))

            def expert_weights(e):
                for area, w, arrived, used in ((gu_stage, w_gu, gu_in, gu_lo), (dn_stage, w_dn, dn_in, dn_lo)):
                    wait(sp, used, e)
                    src = w[e] if isinstance(e, int) else w[bass.ds(e, 1), :, :].rearrange("a p s -> p (a s)")
                    sp.dma_start(area, src).then_inc(arrived, 16)

            expert_weights(0)
            with sp.Fori(1, E) as e:
                expert_weights(e)
            for t in range(NT):
                sp.wait_ge(y_added, NT * (E - 1) + t + 1)
                sp.dma_start(out_tiles[0][:, t, :], x_sb[:, 0, t, :]).then_inc(stored, 16)
            sp.wait_ge(stored, 16 * (B - 1 + NT))

        @block.tensor
        def _(pe):
            def product(dst, left, right, first=True, last=True):
                (lh, ll), (rh, rl) = left, right
                pe.matmul(dst, lh, rl, start=first, stop=False)
                pe.matmul(dst, lh, rh, start=False, stop=False)
                return pe.matmul(dst, ll, rh, start=False, stop=last)

            def turn(n, tile, ready, count):
                pe.wait_ge(ready, count)
                wait(pe, turned_lo, n - 1)
                for j in range(4):
                    last = pe.transpose(t_bank[n % 2][:, j * P:(j + 1) * P], tile[:, j * P:(j + 1) * P], ident[:])
                last.then_inc(turned, 1)

            pe.wait_ge(ident_ready, 2)
            for kind, b in L0_ORDER:
                if kind in "ADF":
                    for i in range(NT):
                        turn(TURN[kind, b] + i, xn[:, i, :], xn_ready, XN[kind.lower(), b] + i + 1)
                elif kind == "P":
                    for i in range(NT):
                        turn(TURN[kind, b] + i, prob[:, i, :], e0_scaled, PROB["S", b] + i + 1)
                elif kind == "Q":
                    pe.wait_ge(split_lo, 2 + b)
                    wait(pe, qk0_lo, 2 * b)
                    for n in range(2):
                        for cj in range(CT):
                            at = (n * CT + cj) * P
                            last = product(j_bank[n][:], [t[:, at:at + P] for t in w0s],
                                           [t[:, b, cj, :] for t in cT], cj == 0, cj == CT - 1)
                        last.then_inc(qk0_mm, 1)
                elif kind == "S":
                    pe.wait_ge(qk0_lo, 2 * (b + 1))
                    for i in range(NT):
                        wait(pe, e0_exp, PROB[kind, b] + i - 1)
                        product(s_bank[i % 2][:], [t[:, 0, i * P:(i + 1) * P] for t in qT],
                                [t[:, 1, :] for t in qT]).then_inc(e0_mm, 1)
                elif kind in "CE":
                    pe.wait_ge(turned_lo, TURN["P" if kind == "C" else "D", b] + 4)
                    if kind == "E":
                        pe.wait_ge(wf_lo, DT)
                    for i in range(NT):
                        n = WIDE[kind, b] + i
                        wait(pe, wide_added, n - 1)
                        right = probT if kind == "C" else wf
                        for j in range(DT):
                            last = product(w_bank[n % 2][:], [t[:, b, j, i * P:(i + 1) * P] for t in xnT],
                                           [t[:, j, :] for t in right], j == 0, j == DT - 1)
                        last.then_inc(wide_mm, 1)

            def step(h, k, proj=True, score=True, value=True):
                def scores(i):
                    if not score:
                        return
                    u = k - 1
                    if i == 0:
                        need(pe, q_lo, 1, h, u, 1)
                        need(pe, kT_lo, 1, h, u, 1)
                    need(pe, p_exp, 4, h, u, i - 1)
                    product(s_bank[i % 2][:], [t[:, u % 2, i * P:(i + 1) * P] for t in qT],
                            [t[:, u % 2, 0, :] for t in kv]).then_inc(s_mm, 1)

                def probs(i):
                    if not score:
                        return
                    u = k - 1
                    need(pe, p_exp, 4, h, u, i + 1)
                    if i == 1:
                        need(pe, q_ss_out, 1, h, u, 1)
                    else:
                        need(pe, p_lo, 4, h, u, (0, None, 1, 3)[i])
                    for j in range(4):
                        last = pe.transpose(t_bank[P_BANK[i]][:, j * P:(j + 1) * P], prob[:, i, j * P:(j + 1) * P],
                                            ident[:])
                    last.then_inc(p_turned, 1)

                def values():
                    if not value:
                        return
                    w = k - 2
                    need(pe, p_lo, 4, h, w, 4)
                    need(pe, v_lo, 1, h, w, 1)
                    need(pe, kv_copied, 2, h, k - 1, 2 if proj else 0)
                    for j in range(NT):
                        last = product(j_bank[0][:], [t[:, w % 2, 1, j * P:(j + 1) * P] for t in kv],
                                       [t[:, j, :] for t in probT], j == 0, j == NT - 1)
                    last.then_inc(pv_mm, 1)

                def project_out(i):
                    if not value:
                        return
                    w = k - 2
                    if i == 0:
                        need(pe, o_lo, 1, h, w, 1)
                        wait(pe, wo_lo, h + (1 if k >= 2 else 0))
                    need(pe, w_added, 4, h, w, i - 1)
                    product(w_bank[i % 2][:], [t[:, i * P:(i + 1) * P] for t in oT],
                            [t[:] for t in wo]).then_inc(w_mm, 1)

                def key_value(half):
                    if not proj:
                        return
                    if half == 0:
                        wait(pe, wkv_lo, h + 1)
                        need(pe, q_lo, 1, h, k - 1, 1)
                        need(pe, q_squared, 2, h, k - 1, 2)
                    else:
                        need(pe, kv_copied, 2, h, k - 1, 2)
                        if value:
                            need(pe, o_lo, 1, h, k - 2, 1)
                    for a in range(2):
                        t0 = (2 * half + a) * P
                        for cj in range(CT):
                            last = product(j_bank[1 - half][:, a * 2 * HD:(a + 1) * 2 * HD],
                                           [t[:, k, cj, t0:t0 + P] for t in cT],
                                           [t[:, cj, :] for t in wkv], cj == 0, cj == CT - 1)
                    last.then_inc(kv_mm, 1)

                def query(tiles):
                    if not proj:
                        return
                    if 0 in tiles:
                        wait(pe, wq_lo, h + 1)
                        need(pe, kv_copied, 2, h, k, 1)
                        if isinstance(h, int) and h == 0:
                            pe.wait_ge(turned_lo, TURN["F", k] + 4)
                    for dj in tiles:
                        last = product(j_bank[1][:], [t[:, dj * HD:(dj + 1) * HD] for t in wq],
                                       [t[:, k, dj, :] for t in xnT], dj == 0, dj == DT - 1)
                    if DT - 1 in tiles:
                        last.then_inc(q_mm, 1)

                def key_turn():
                    if not proj:
                        return
                    need(pe, k_scaled, 1, h, k, 1)
                    if score:
                        need(pe, p_lo, 4, h, k - 1, 2)
                    else:
                        pe.wait_ge(turned_lo, TURNS)
                    for j in range(NT):
                        last = pe.transpose(t_bank[0][:, j * P:(j + 1) * P], kv_raw[:, j, 0:HD], ident[:])
                    last.then_inc(kT_mm, 1)

                def query_squares():
                    if not score:
                        return
                    u = k - 1
                    need(pe, sq_lo, 1, h, u, 1)
                    need(pe, kT_lo, 1, h, u, 1)
                    for i in range(NT):
                        here = slice(i * P, (i + 1) * P)
                        pe.matmul(t_bank[0][:, 2 * i:2 * i + 2], sqs[0][:, here], ones[:], start=True, stop=False)
                        last = pe.matmul(t_bank[0][:, 2 * i:2 * i + 2], sqs[1][:, here], ones[:], start=False,
                                         stop=True)
                    last.then_inc(q_ss_mm, 1)

                scores(0)
                scores(1)
                query_squares()
                values()
                key_value(0)
                probs(0)
                scores(2)
                key_value(1)
                project_out(0)
                scores(3)
                probs(1)
                query((0, 1))
                probs(2)
                query((2, 3))
                project_out(1)
                key_turn()
                probs(3)
                project_out(2)
                project_out(3)

            pe.wait_ge(const_ready, 2)
            step(0, 0, score=False, value=False)
            step(0, 1, value=False)
            step(0, 2)
            step(0, 3)
            with pe.Fori(1, H) as h:
                for k in range(B):
                    step(h, k)
            step(H, 0, proj=False)
            step(H, 1, proj=False, score=False)

            for i in range(NT):
                turn(TURNS + i, xn[:, i, :], xn_ready, XNS + i + 1)

            def expert_step(it, k, up=True, down=True):
                def gate_up(j):
                    if not up:
                        return
                    bank = (3 * k + j) % 2
                    if j == 0:
                        need_e(pe, gu_lo, 1, it, k, 1)
                    need_e(pe, silu_ready, IT, it, k, j - 1)
                    for dj in range(DT):
                        last = product(s_bank[bank][0:IW[j], :], [cols(a, 0, dj, j) for a in gu_w[k % 2]],
                                       [t[:, 0, dj, :] for t in xnT], dj == 0, dj == DT - 1)
                    last.then_inc(g_mm, 1)
                    need_e(pe, h_ready, IT, it, k, j - 1)
                    for dj in range(DT):
                        last = product(t_bank[bank][0:IW[j], :], [cols(a, 1, dj, j) for a in gu_w[k % 2]],
                                       [t[:, 0, dj, :] for t in xnT], dj == 0, dj == DT - 1)
                    last.then_inc(u_mm, 1)

                def project_down(t):
                    if not down:
                        return
                    e = k - 1
                    if t == 0:
                        need_e(pe, h_hi, IT, it, e, IT)
                        need_e(pe, h_lo, IT, it, e, IT)
                        need_e(pe, dn_lo, 1, it, e, 1)
                    need_e(pe, y_added, NT, it, e, t - 1)
                    for j in range(IT):
                        last = product(w_bank[t % 2][:], [a[0:IW[j], j, t * P:(t + 1) * P] for a in hT[e % 2]],
                                       [a[0:IW[j], j * D:(j + 1) * D] for a in dn_w[e % 2]], j == 0, j == IT - 1)
                    last.then_inc(d_mm, 1)

                gate_up(0)
                project_down(0)
                project_down(1)
                gate_up(1)
                project_down(2)
                gate_up(2)
                project_down(3)

            pe.wait_ge(turned_lo, TURNS + NT)
            expert_step(0, 0, down=False)
            expert_step(0, 1)
            with pe.Fori(1, E // 2) as it:
                expert_step(it, 0)
                expert_step(it, 1)
            expert_step(E // 2, 0, up=False)

        @block.scalar
        def _(act):
            def copy_hi(dst, src):
                return nc.scalar.copy(dst, src)

            def turned_tile(kind, b, i, n):
                act.wait_ge(turned, n + 1)
                dst = probT[0][:, :, i * P:(i + 1) * P] if kind == "P" else xnT[0][:, b, :, i * P:(i + 1) * P]
                copy_hi(dst, t_bank[n % 2][:].rearrange("p (j q) -> p j q", j=4)).then_inc(turned_hi, 1)

            act.wait_ge(vec_in, 16)
            nc.scalar.activation(tanh_g[:], vec[:, G_X:G_X + 4], ACT.Tanh).then_inc(gates_tanh, 1)
            nc.scalar.activation(small[:, 0:NBITS], vec[:, MASK:MASK + NBITS], ACT.Tanh, scale=0.5).then_inc(
                mask_tanh, 1)
            for kind, b in L0_ORDER:
                if kind == "K":
                    act.wait_ge(split_in[b], 16)
                    copy_hi(w0s[0][:] if b == 0 else cT[0][:, b - 1, :, :], split_stage[b]).then_inc(split_hi, 1)
                elif kind in "ADF":
                    for i in range(NT):
                        turned_tile(kind, b, i, TURN[kind, b] + i)
                elif kind == "Q":
                    for n, bias in enumerate((BQ, BK)):
                        act.wait_ge(qk0_mm, 2 * b + n + 1)
                        wait(act, e0_mm, 4 * b)
                        nc.scalar.activation(qT[0][:, n, :], j_bank[n][:], ACT.Identity,
                                             bias=vec[:, bias:bias + 1]).then_inc(qk0_hi, 1)
                elif kind == "S":
                    def scaled(i):
                        act.wait_ge(e0_inv, PROB[kind, b] + i + 1)
                        nc.scalar.mul(prob[:, i, :], prob[:, i, :], inv_sum[:, b % 2, i:i + 1]).then_inc(e0_scaled, 1)

                    for i in range(NT):
                        n = PROB[kind, b] + i
                        act.wait_ge(e0_max, n + 1)
                        if b:
                            act.wait_ge(turned, TURN["P", b - 1] + i + 1)
                        nc.scalar.activation(prob[:, i, :], s_bank[i % 2][:], ACT.Exp, bias=neg_max[:, b % 2, i:i + 1],
                                             accum_out=row_sum[:, b % 2, i:i + 1]).then_inc(e0_exp, 1)
                        if i:
                            scaled(i - 1)
                    scaled(NT - 1)
                elif kind == "P":
                    for i in range(NT):
                        turned_tile(kind, b, i, TURN[kind, b] + i)
                elif kind == "G":
                    act.wait_ge(planes_in[b % 2], 16 * (b // 2 + 1))
                    at = 2 * (b % 2)
                    if b < DT * NBITS:
                        nc.scalar.activation(stage[:, at:at + 2, :], stage[:, at:at + 2, :], ACT.Tanh,
                                             scale=0.5).then_inc(bit_tanh, 1)
                        if b % NBITS == NBITS - 1:
                            act.wait_ge(bit_added, b + 1)
                            copy_hi(wf[0][:, b // NBITS, :], bit_acc).then_inc(wf_hi, 1)

            def step(h, k, proj=True, score=True, value=True):
                def softmax(i):
                    if not score:
                        return
                    u = k - 1
                    need(act, s_max, 4, h, u, i + 1)
                    need(act, p_turned, 4, h, u - 1, i + 1)
                    nc.scalar.activation(prob[:, i, :], s_bank[i % 2][:], ACT.Exp,
                                         bias=neg_bias[:, u % 2, i:i + 1], scale=q_scale[:, u % 2, i:i + 1],
                                         accum_out=row_sum[:, u % 2, i:i + 1]).then_inc(p_exp, 1)

                def probs_hi(i):
                    if not score:
                        return
                    need(act, p_turned, 4, h, k - 1, i + 1)
                    copy_hi(probT[0][:, :, i * P:(i + 1) * P],
                            t_bank[P_BANK[i]][:].rearrange("p (j q) -> p j q", j=4)).then_inc(p_hi, 1)

                def key_value_rows(half):
                    if not proj:
                        return
                    need(act, kv_mm, 2, h, k, half + 1)
                    if half == 0:
                        need(act, kT_mm, 1, h, k - 1, 1)
                        need(act, v_lo, 1, h, k - 1, 1)
                    nc.scalar.copy(kv_raw[:, 2 * half:2 * half + 2, :],
                                   j_bank[1 - half][:].rearrange("p (a c) -> p a c", a=2)).then_inc(kv_copied, 1)

                if k == 0 and proj:
                    wait(act, wkv_in, h * 16 + 16)
                    need(act, kv_mm, 2, h, -1, 2)
                    copy_hi(wkv[0][:, :, :].rearrange("p a c -> p (a c)"), stage[:, 0, :]).then_inc(wkv_hi, 1)
                if k == 2:
                    wait(act, wo_in, h * 16 + 16)
                    need(act, w_mm, 4, h, -1, 4)
                    copy_hi(wo[0][:], stage[:, 2, :]).then_inc(wo_hi, 1)
                softmax(0)
                if k == 0 and proj:
                    wait(act, wq_in, h * 16 + 16)
                    need(act, q_mm, 1, h, -1, 1)
                    copy_hi(wq[0][:], stage[:, 1, :]).then_inc(wq_hi, 1)
                if value:
                    need(act, pv_mm, 1, h, k - 2, 1)
                    need(act, w_mm, 4, h, k - 3, 4)
                    copy_hi(oT[0][:], j_bank[0][:]).then_inc(o_hi, 1)
                softmax(1)
                key_value_rows(0)
                probs_hi(0)
                key_value_rows(1)
                if proj:
                    need(act, kv_copied, 2, h, k, 2)
                    need(act, k_scaled, 1, h, k - 1, 1)
                    for i in range(NT):
                        nc.scalar.activation(ksq[:, i, :], kv_raw[:, i, 0:HD], ACT.Square, scale=HD ** -0.5,
                                             accum_out=k_ss[:, i:i + 1]).then_inc(k_squares, 1)
                softmax(2)
                softmax(3)
                probs_hi(1)
                probs_hi(2)
                if proj:
                    need(act, q_mm, 1, h, k, 1)
                    need(act, s_mm, 4, h, k - 2, 4)
                    copy_hi(qT[0][:, k % 2, :], j_bank[1][:]).then_inc(q_hi, 1)
                    need(act, kT_mm, 1, h, k, 1)
                    nc.scalar.activation(kv[0][:, k % 2, 0, :], t_bank[0][:], ACT.Copy,
                                         scale=gain[:]).then_inc(kT_hi, 1)
                    need(act, q_lo, 1, h, k, 1)
                    need(act, q_ss_mm, 1, h, k - 1, 1)
                    nc.scalar.activation(sqs[0][:], j_bank[1][:], ACT.Square).then_inc(q_squared, 1)
                    need(act, sq_lo, 1, h, k - 1, 1)
                    nc.scalar.activation(sq[:], j_bank[1][:], ACT.Square).then_inc(q_squared, 1)
                probs_hi(3)

            act.wait_ge(gain_ready, 1)
            step(0, 0, score=False, value=False)
            step(0, 1, value=False)
            step(0, 2)
            step(0, 3)
            with act.Fori(1, H) as h:
                for k in range(B):
                    step(h, k)
            step(H, 0, proj=False)
            step(H, 1, proj=False, score=False)

            for i in range(NT):
                turned_tile("M", 0, i, TURNS + i)

            def gate_up_hi(it, k):
                need_e(act, gu_in, 16, it, k, 16)
                need_e(act, u_mm, IT, it, k - 2, IT)
                copy_hi(gu_w[k % 2][0], gu_stage).then_inc(gu_hi, 1)

            def expert_step(it, k, more=True):
                def silu(j):
                    need_e(act, g_mm, IT, it, k, j + 1)
                    need_e(act, h_ready, IT, it, k, j - 1)
                    g = (IT * k + j) % 2
                    nc.scalar.activation(prob[0:IW[j], g, :], s_bank[g][0:IW[j], :], ACT.Silu).then_inc(silu_ready, 1)

                def inner_hi(j):
                    need_e(act, h_ready, IT, it, k, j + 1)
                    if j == 0:
                        need_e(act, d_mm, NT, it, k - 2, NT)
                    copy_hi(hT[k % 2][0][0:IW[j], j, :],
                            prob[0:IW[j], 2 + (IT * k + j) % 2, :]).then_inc(h_hi, 1)

                silu(0)
                need_e(act, dn_in, 16, it, k, 16)
                need_e(act, d_mm, NT, it, k - 2, NT)
                copy_hi(dn_w[k % 2][0], dn_stage).then_inc(dn_hi, 1)
                inner_hi(0)
                silu(1)
                if more:
                    gate_up_hi(it, k + 1)
                inner_hi(1)
                silu(2)
                inner_hi(2)

            act.wait_ge(q_mm, B * H)
            act.wait_ge(kv_mm, 2 * B * H)
            gate_up_hi(0, 0)
            expert_step(0, 0)
            expert_step(0, 1)
            with act.Fori(1, E // 2 - 1) as it:
                expert_step(it, 0)
                expert_step(it, 1)
            expert_step(E // 2 - 1, 0)
            expert_step(E // 2 - 1, 1, more=False)

        @block.vector
        def _(dve):
            done, tiles_seen = [0], [0]

            def then_wait(ins):
                done[0] += 1
                ins.then_inc(dve_own, 1)
                dve.wait_ge(dve_own, done[0])

            def lower(dst, src, hi):
                return nc.vector.tensor_tensor(dst, src, hi, ALU.subtract)

            def tile_moments(b, i):
                n = tiles_seen[0]
                tiles_seen[0] += 1
                wait(dve, moments, n - 3)
                then_wait(nc.vector.bn_stats(stats[:, n % 4, :], x_sb[:, b, i, :]))
                nc.vector.bn_aggr(mean_var[:, b, i, :], stats[:, n % 4, :]).then_inc(moments, 1)

            def turned_tile(kind, b, i, n):
                dve.wait_ge(turned_hi, n + 1)
                where = [t[:, :, i * P:(i + 1) * P] if kind == "P" else t[:, b, :, i * P:(i + 1) * P]
                         for t in (probT if kind == "P" else xnT)]
                lower(where[1], t_bank[n % 2][:].rearrange("p (j q) -> p j q", j=4), f32(where[0])).then_inc(
                    turned_lo, 1)

            nc.vector.memset(f32(ones[:]), 1.0).then_inc(const_ready, 1)
            nc.vector.memset(minus_half[:], -0.5).then_inc(const_ready, 1)
            nc.vector.memset(eps[:], EPS).then_inc(const_ready, 1)
            dve.wait_ge(vec_in, 16)
            nc.vector.tensor_tensor(gain[:], vec[:, GQ:GQ + 1], vec[:, GK:GK + 1], ALU.mult).then_inc(gain_ready, 1)
            dve.wait_ge(gates_tanh, 1)
            dve.wait_ge(mask_tanh, 1)
            then_wait(nc.vector.tensor_scalar(small[:, 4:8], small[:, 0:4], 0.5, 0.5, ALU.mult, ALU.add))
            then_wait(nc.vector.tensor_tensor(small[:, 0:4], small[:, 4:8], vec[:, EXPS:EXPS + NBITS], ALU.mult))
            then_wait(nc.vector.tensor_scalar(small[:, 4:8], small[:, 0:4], vec[:, SCALE:SCALE + 1],
                                              tanh_g[:, 2:3], ALU.mult, ALU.mult))
            then_wait(nc.vector.tensor_scalar(bit_w[:], small[:, 4:8], 0.5, None, ALU.mult))

            def norm(b, group, freed):
                dve.wait_ge(rstd_ready, group + 1)
                for i in range(NT):
                    if freed is not None:
                        dve.wait_ge(turned, freed + i + 1)
                    nc.vector.tensor_scalar(xn[:, i, :], x_sb[:, b, i, :], mean_var[:, b, i, 0:1],
                                            rstd[:, b, i:i + 1], ALU.subtract, ALU.mult).then_inc(xn_ready, 1)

            last_turn = None
            for kind, b in L0_ORDER:
                if kind in "ADF":
                    for i in range(NT):
                        turned_tile(kind, b, i, TURN[kind, b] + i)
                elif kind == "m":
                    dve.wait_ge(x_in[b], 16)
                    for i in range(NT):
                        tile_moments(b, i)
                elif kind in "adf":
                    of = {"a": "m", "d": "C", "f": "E"}[kind]
                    norm(b, MOMENTS[of, b] // NT, last_turn)
                    last_turn = TURN[kind.upper(), b]
                elif kind == "Q":
                    for n, bias in enumerate((BQ, BK)):
                        dve.wait_ge(qk0_hi, 2 * b + n + 1)
                        nc.vector.scalar_tensor_tensor(
                            out=qT[1][:, n, :], in0=j_bank[n][:], scalar=vec[:, bias:bias + 1],
                            in1=f32(qT[0][:, n, :]), op0=ALU.add, op1=ALU.subtract).then_inc(qk0_lo, 1)
                elif kind == "S":
                    def inverse(i):
                        dve.wait_ge(e0_exp, PROB[kind, b] + i + 1)
                        nc.vector.reciprocal(inv_sum[:, b % 2, i:i + 1], row_sum[:, b % 2, i:i + 1]).then_inc(
                            e0_inv, 1)
                    for i in range(NT):
                        dve.wait_ge(e0_mm, PROB[kind, b] + i + 1)
                        nc.vector.tensor_reduce(neg_max[:, b % 2, i:i + 1], s_bank[i % 2][:], AX_X, ALU.max,
                                                negate=True).then_inc(e0_max, 1)
                        if i:
                            inverse(i - 1)
                    inverse(NT - 1)
                elif kind == "P":
                    for i in range(NT):
                        turned_tile(kind, b, i, TURN[kind, b] + i)
                elif kind in "CE":
                    for i in range(NT):
                        n = WIDE[kind, b] + i
                        dve.wait_ge(wide_mm, n + 1)
                        here = x_sb[:, b, i, :]
                        if kind == "C":
                            nc.vector.scalar_tensor_tensor(
                                out=here, in0=w_bank[n % 2][:], scalar=tanh_g[:, 0:1], in1=here,
                                op0=ALU.mult, op1=ALU.add).then_inc(wide_added, 1)
                        else:
                            dve.wait_ge(bias_added, NT * b + i + 1)
                            nc.vector.tensor_tensor(here, w_bank[n % 2][:], here, ALU.add).then_inc(wide_added, 1)
                        dve.wait_ge(wide_added, n + 1)
                        tile_moments(b, i)
                elif kind == "G":
                    j, n = divmod(b, NBITS)
                    at = 2 * (b % 2)
                    factor = bit_w[:, n:n + 1] if j < DT else vec[:, BEXPS + n:BEXPS + n + 1]
                    dve.wait_ge(bit_diff, b + 1)
                    if n == 0:
                        wait(dve, wf_lo, j)
                        nc.vector.tensor_scalar(bit_acc, stage[:, at, :], factor, None, ALU.mult).then_inc(
                            bit_added, 1)
                    else:
                        nc.vector.scalar_tensor_tensor(out=bit_acc, in0=stage[:, at, :], scalar=factor, in1=bit_acc,
                                                       op0=ALU.mult, op1=ALU.add).then_inc(bit_added, 1)
                    dve.wait_ge(bit_added, b + 1)
                    if b == NBIT_CHUNKS - 1:
                        steps = float(2 ** NBITS - 1)
                        then_wait(nc.vector.tensor_scalar(bias_t, bit_acc, -1.0, 1.0, ALU.max, ALU.min))
                        then_wait(nc.vector.tensor_scalar(bias_t, bias_t, steps, None, ALU.mult))
                        then_wait(nc.vector.tensor_scalar(bias_t, bias_t, ROUND, None, ALU.add))
                        then_wait(nc.vector.tensor_scalar(bias_t, bias_t, -ROUND, 1.0 / steps, ALU.add, ALU.mult))
                        nc.vector.tensor_scalar(bias_t, bias_t, vec[:, BSCALE:BSCALE + 1], tanh_g[:, 2:3],
                                                ALU.mult, ALU.mult).then_inc(bias_ready, 1)

            dve.wait_ge(idx_in, 32)
            then_wait(nc.vector.tensor_copy(idx_f[:], idx[:]))
            for e in range(E):
                then_wait(nc.vector.scalar_tensor_tensor(
                    out=picked[:], in0=idx_f[:], scalar=float(e), in1=topw[:], op0=ALU.is_equal, op1=ALU.mult))
                then_wait(nc.vector.tensor_reduce(share[:, :, e:e + 1], picked[:], AX_X, ALU.add))
            then_wait(nc.vector.tensor_scalar(share[:], share[:], tanh_g[:, 3:4], None, ALU.mult))

            own_max, own_inv = sem("own_max"), sem("own_inv")

            def step(h, k, proj=True, score=True, value=True):
                def maximum(i):
                    if not score:
                        return
                    u = k - 1
                    need(dve, s_mm, 4, h, u, i + 1)
                    nc.vector.tensor_reduce(neg_max[:, u % 2, i:i + 1], s_bank[i % 2][:], AX_X, ALU.max,
                                            negate=True).then_inc(own_max, 1)

                def shift(i):
                    if not score:
                        return
                    u = k - 1
                    if i == 0:
                        need(dve, q_scale_ready, 1, h, u, 1)
                    need(dve, own_max, 4, h, u, i + 1)
                    nc.vector.tensor_tensor(neg_bias[:, u % 2, i:i + 1], neg_max[:, u % 2, i:i + 1],
                                            q_scale[:, u % 2, i:i + 1], ALU.mult).then_inc(s_max, 1)

                def probs_lo(i):
                    if not score:
                        return
                    need(dve, p_hi, 4, h, k - 1, i + 1)
                    hi, lo = [t[:, :, i * P:(i + 1) * P] for t in probT]
                    lower(lo, t_bank[P_BANK[i]][:].rearrange("p (j q) -> p j q", j=4), f32(hi)).then_inc(p_lo, 1)

                def add(i):
                    if not value:
                        return
                    w = k - 2
                    need(dve, w_mm, 4, h, w, i + 1)
                    if i == 0:
                        need(dve, own_inv, 2, h, w, 2)
                    here = x_sb[:, w % B, i, :]
                    nc.vector.scalar_tensor_tensor(out=here, in0=w_bank[i % 2][:], scalar=inv_sum[:, w % 2, i:i + 1],
                                                   in1=here, op0=ALU.mult, op1=ALU.add).then_inc(w_added, 1)

                maximum(0)
                maximum(1)
                if score:
                    need(dve, q_ss_mm, 1, h, k - 1, 1)
                    nc.vector.tensor_scalar(q_ss[:, (k - 1) % 2, :], t_bank[0][:, 0:2 * NT:2], HD * EPS, None,
                                            ALU.add).then_inc(q_ss_out, 1)
                shift(0)
                shift(1)
                if value:
                    w = k - 2
                    nc.vector.reciprocal(inv_sum[:, w % 2, :], row_sum[:, w % 2, :]).then_inc(own_inv, 1)
                    need(dve, own_inv, 2, h, w, 1)
                    nc.vector.tensor_scalar(inv_sum[:, w % 2, :], inv_sum[:, w % 2, :], tanh_g[:, 1:2], None,
                                            ALU.mult).then_inc(own_inv, 1)
                    need(dve, o_hi, 1, h, w, 1)
                    lower(oT[1][:], j_bank[0][:], f32(oT[0][:])).then_inc(o_lo, 1)
                probs_lo(0)
                maximum(2)
                shift(2)
                if proj:
                    need(dve, kv_copied, 2, h, k, 2)
                    need(dve, pv_mm, 1, h, k - 2, 1)
                    nc.vector.tensor_copy(kv[0][:, k % 2, 1, :].rearrange("p (j c) -> p j c", j=NT),
                                          kv_raw[:, :, HD:2 * HD]).then_inc(v_hi, 1)
                add(0)
                maximum(3)
                shift(3)
                probs_lo(1)
                probs_lo(2)
                if proj:
                    need(dve, q_hi, 1, h, k, 1)
                    lower(qT[1][:, k % 2, :], j_bank[1][:], f32(qT[0][:, k % 2, :])).then_inc(q_lo, 1)
                add(1)
                if proj:
                    need(dve, kT_hi, 1, h, k, 1)
                    nc.vector.scalar_tensor_tensor(
                        out=kv[1][:, k % 2, 0, :], in0=t_bank[0][:], scalar=gain[:], in1=f32(kv[0][:, k % 2, 0, :]),
                        op0=ALU.mult, op1=ALU.subtract).then_inc(kT_lo, 1)
                probs_lo(3)
                add(2)
                add(3)

            step(0, 0, score=False, value=False)
            step(0, 1, value=False)
            step(0, 2)
            step(0, 3)
            with dve.Fori(1, H) as h:
                for k in range(B):
                    step(h, k)
            dve.wait_ge(w_added, 4 * (B * (H - 1) + 1))
            for i in range(NT):
                tile_moments(0, i)
            dve.wait_ge(sq_lo, B * H)
            dve.wait_ge(k_squares, 4 * B * H)
            norm(0, NMOMENTS // NT, last_turn)
            step(H, 0, proj=False)
            step(H, 1, proj=False, score=False)
            for i in range(NT):
                turned_tile("M", 0, i, TURNS + i)

            def expert_step(it, k, up=True, down=True):
                def inner(j):
                    if not up:
                        return
                    g = (IT * k + j) % 2
                    need_e(dve, silu_ready, IT, it, k, j + 1)
                    need_e(dve, u_mm, IT, it, k, j + 1)
                    need_e(dve, h_lo, IT, it, k, j - 1)
                    nc.vector.tensor_tensor(prob[0:IW[j], 2 + g, :], t_bank[g][0:IW[j], :], prob[0:IW[j], g, :],
                                            ALU.mult).then_inc(h_ready, 1)

                def add(t):
                    if not down:
                        return
                    e = k - 1
                    need_e(dve, d_mm, NT, it, e, t + 1)
                    here = x_sb[:, 0, t, :]
                    at = it * 2 + e
                    factor = share[:, t, at:at + 1] if isinstance(at, int) else share[:, t, bass.ds(at, 1)]
                    nc.vector.scalar_tensor_tensor(out=here, in0=w_bank[t % 2][:], scalar=factor, in1=here,
                                                   op0=ALU.mult, op1=ALU.add).then_inc(y_added, 1)

                inner(0)
                add(0)
                add(1)
                inner(1)
                add(2)
                inner(2)
                add(3)

            expert_step(0, 0, down=False)
            expert_step(0, 1)
            with dve.Fori(1, E // 2) as it:
                expert_step(it, 0)
                expert_step(it, 1)
            expert_step(E // 2, 0, up=False)

        @block.gpsimd
        def _(pool):
            done = [0]

            def then_wait(ins):
                done[0] += 1
                ins.then_inc(pool_own, 1)
                pool.wait_ge(pool_own, done[0])

            def lower(dst, src, hi):
                return nc.gpsimd.tensor_tensor(dst, src, hi, ALU.subtract)

            def inverse_deviations(n, b):
                pool.wait_ge(moments, NT * (n + 1))
                wait(pool, rstd_ready, n)
                nc.gpsimd.tensor_tensor(var_eps[:], mean_var[:, b, :, 1], eps[:], ALU.add).then_inc(var_ready, 1)
                pool.wait_ge(var_ready, n + 1)
                nc.gpsimd.tensor_tensor(rstd[:, b, :], var_eps[:], minus_half[:], ALU.pow).then_inc(
                    rstd_ready, 1)

            nc.gpsimd.memset(ident[:], 0.0).then_inc(ident_ready, 1)
            pool.wait_ge(ident_ready, 1)
            nc.gpsimd.affine_select(out=ident[:], in_=ident[:], compare_op=ALU.not_equal, fill=1.0, base=0,
                                    pattern=[[-1, P]], channel_multiplier=1).then_inc(ident_ready, 1)
            pool.wait_ge(const_ready, 3)
            for kind, b in L0_ORDER:
                if kind == "K":
                    pool.wait_ge(split_hi, b + 1)
                    hi, lo = [t[:] if b == 0 else t[:, b - 1, :, :] for t in (w0s if b == 0 else cT)]
                    lower(lo, split_stage[b], f32(hi)).then_inc(split_lo, 1)
                elif kind in "mCE":
                    inverse_deviations(MOMENTS[kind, b] // NT, b)
                elif kind == "B":
                    pool.wait_ge(bias_ready, 1)
                    pool.wait_ge(xn_ready, XN["d", b] + NT)
                    for i in range(NT):
                        nc.gpsimd.tensor_tensor(x_sb[:, b, i, :], x_sb[:, b, i, :], bias_t,
                                                ALU.add).then_inc(bias_added, 1)
                elif kind == "G":
                    at = 2 * (b % 2)
                    if b < DT * NBITS:
                        pool.wait_ge(bit_tanh, b + 1)
                    else:
                        pool.wait_ge(planes_in[b % 2], 16 * (b // 2 + 1))
                    nc.gpsimd.tensor_tensor(stage[:, at, :], stage[:, at, :], stage[:, at + 1, :],
                                            ALU.subtract).then_inc(bit_diff, 1)
                    if b < DT * NBITS and b % NBITS == NBITS - 1:
                        pool.wait_ge(wf_hi, b // NBITS + 1)
                        lower(wf[1][:, b // NBITS, :], bit_acc, f32(wf[0][:, b // NBITS, :])).then_inc(wf_lo, 1)

            def lower_weights(dst, slot, h, hi_done, lo_done):
                hi, lo = dst
                wait(pool, hi_done, h + 1)
                lower(lo, stage[:, slot, :], f32(hi)).then_inc(lo_done, 1)

            k_own = sem("k_own")

            def query_scale(h, u):
                need(pool, q_ss_out, 1, h, u, 1)
                nc.gpsimd.tensor_tensor(q_scale[:, u % 2, :], q_ss[:, u % 2, :], minus_half[:],
                                        ALU.pow).then_inc(q_scale_ready, 1)

            def step(h, k, score=True):
                if k == 0:
                    lower_weights([t[:, :, :].rearrange("p a c -> p (a c)") for t in wkv], 0, h, wkv_hi, wkv_lo)
                if score:
                    query_scale(h, k - 1)
                if k == 0:
                    lower_weights([t[:] for t in wq], 1, h, wq_hi, wq_lo)
                if k == 2:
                    lower_weights([t[:] for t in wo], 2, h, wo_hi, wo_lo)
                need(pool, k_squares, 4, h, k, 4)
                nc.gpsimd.tensor_tensor(k_ms[:], k_ss[:], eps[:], ALU.add).then_inc(k_own, 1)
                need(pool, k_own, 2, h, k, 1)
                nc.gpsimd.tensor_tensor(k_rs[:], k_ms[:], minus_half[:], ALU.pow).then_inc(k_own, 1)
                need(pool, k_own, 2, h, k, 2)
                keys = kv_raw[:, :, 0:HD]
                nc.gpsimd.tensor_tensor(keys, keys, k_rs[:].unsqueeze(2).to_broadcast([P, NT, HD]),
                                        ALU.mult).then_inc(k_scaled, 1)
                hi, lo = [t[:, k % 2, 1, :].rearrange("p (j c) -> p j c", j=NT) for t in kv]
                need(pool, v_hi, 1, h, k, 1)
                lower(lo, kv_raw[:, :, HD:2 * HD], f32(hi)).then_inc(v_lo, 1)
                need(pool, q_squared, 2, h, k, 2)
                lower(sqs[1][:], sq[:], f32(sqs[0][:])).then_inc(sq_lo, 1)

            step(0, 0, score=False)
            for k in range(1, B):
                step(0, k)
            with pool.Fori(1, H) as h:
                for k in range(B):
                    step(h, k)
            inverse_deviations(NMOMENTS // NT, 0)
            query_scale(H, -1)

            def gate_up_lo(it, k):
                need_e(pool, gu_hi, 1, it, k, 1)
                lower(gu_w[k % 2][1], gu_stage, f32(gu_w[k % 2][0])).then_inc(gu_lo, 1)

            def expert_step(it, k, more=True):
                def inner_lo(j):
                    need_e(pool, h_hi, IT, it, k, j + 1)
                    lower(hT[k % 2][1][0:IW[j], j, :], prob[0:IW[j], 2 + (IT * k + j) % 2, :],
                          f32(hT[k % 2][0][0:IW[j], j, :])).then_inc(h_lo, 1)

                need_e(pool, dn_hi, 1, it, k, 1)
                lower(dn_w[k % 2][1], dn_stage, f32(dn_w[k % 2][0])).then_inc(dn_lo, 1)
                inner_lo(0)
                if more:
                    gate_up_lo(it, k + 1)
                inner_lo(1)
                inner_lo(2)

            gate_up_lo(0, 0)
            expert_step(0, 0)
            expert_step(0, 1)
            with pool.Fori(1, E // 2 - 1) as it:
                expert_step(it, 0)
                expert_step(it, 1)
            expert_step(E // 2 - 1, 0)
            expert_step(E // 2 - 1, 1, more=False)


def kernel(**inputs):
    import numpy as np
    import concourse.bacc as bacc
    from concourse.bass_utils import run_bass_kernel_spmd

    a = {name: np.asarray(value) for name, value in inputs.items()}

    def whole(v):
        return np.ascontiguousarray(v)

    ctxT = a["ctx_1024"].transpose(0, 2, 1).reshape(B, CT, P, S)
    columns = [a["L0_xattn_bq"], a["L0_xattn_bk"], a["L1_xattn_gq"], a["L1_xattn_gk"]]
    for name in ("g_xattn", "g_ffn", "L0_ffn_exps", "L0_ffn_bexps", "L0_ffn_mask_weight", "L0_ffn_scale",
                 "L0_ffn_biasscale"):
        columns += [np.broadcast_to(v, (P,)) for v in a[name]]
    vecs = np.stack(columns, axis=1)
    w0 = np.stack([a[n].T.reshape(CT, P, P).transpose(1, 0, 2) for n in ("L0_xattn_Wq", "L0_xattn_Wk")], axis=1)
    planes = np.stack([a[n].transpose(2, 1, 0).reshape(NBITS, DT, P, D) for n in ("L0_ffn_pweight", "L0_ffn_nweight")],
                      axis=2).transpose(1, 0, 2, 3, 4)
    bias = np.stack([np.broadcast_to(a[n].T[:, None, :], (NBITS, P, D)) for n in ("L0_ffn_pbias", "L0_ffn_nbias")],
                    axis=1)
    bits = np.concatenate([planes.reshape(DT * NBITS, 2, P, D), bias], axis=0)
    wk, wv = (a[n].reshape(CT, P, H, HD).transpose(2, 1, 0, 3) for n in ("L1_xattn_Wk", "L1_xattn_Wv"))
    wkv = np.stack([wk, wv], axis=3).reshape(H, P, CT * 2 * HD)
    wq = a["L1_xattn_Wq"].reshape(DT, P, H, HD).transpose(2, 1, 0, 3).reshape(H, P, DT * HD)
    w1 = np.stack([wkv, wq, a["L1_xattn_Wo"].reshape(H, HD, D)], axis=0)
    w_gu = np.stack([a[n].transpose(0, 2, 1).reshape(E, DT, P, I).transpose(0, 2, 1, 3)
                     for n in ("L1_ffn_gate_weight", "L1_ffn_up_weight")], axis=2).reshape(E, P, 2 * DT * I)
    down = np.zeros((E, IT * P, D), a["L1_ffn_down_weight"].dtype)
    down[:, :I] = a["L1_ffn_down_weight"].transpose(0, 2, 1)
    w_dn = down.reshape(E, IT, P, D).transpose(0, 2, 1, 3).reshape(E, P, IT * D)

    def by_tile(v):
        return v.reshape(NT, P, TOPK).transpose(1, 0, 2)

    arrays = {
        "x": a["x"].reshape(B * S, D), "ctxT": ctxT, "vecs": vecs, "w0": w0.reshape(P, 2 * CT * P), "bits": bits,
        "w1": w1, "w_gu": w_gu, "w_dn": w_dn, "topk_idx": by_tile(a["L1_ffn_topk_idx"]),
        "topk_w": by_tile(a["L1_ffn_topk_weight"]),
    }
    arrays = {name: whole(v) for name, v in arrays.items()}
    nc = bacc.Bacc("TRN2", target_bir_lowering=False, num_devices=1, dynamic_dma_scratch_size=4096)
    args = [nc.dram_tensor(name, v.shape, mybir.dt.from_np(v.dtype), kind="ExternalInput").ap()
            for name, v in arrays.items()]
    out = nc.dram_tensor("out", (B * S, D), F32, kind="ExternalOutput").ap()
    flamingo_kernel(nc, *args, out)
    result = run_bass_kernel_spmd(nc, [arrays], core_ids=[0])
    return result.results[0]["out"].reshape(B, S, D)
```

```python
from contextlib import ExitStack

import concourse.bass as bass
from concourse import mybir

F32 = mybir.dt.float32
F32R = mybir.dt.float32r
I32 = mybir.dt.int32
ALU = mybir.AluOpType
ACT = mybir.ActivationFunctionType
AX_X = mybir.AxisListType.X

P = 128
B, S, D, C = 4, 512, 512, 256
NT = S // P
DT = D // P
CT = C // P
H, HD = 16, 128
NBITS = 4
E, I, TOPK = 16, 352, 4
IT = -(-I // P)
IW = [min(P, I - P * j) for j in range(IT)]
EPS = 1e-5
ROUND = 1.5 * 2.0 ** 23

BQ, BK, GQ, GK = range(4)
G_X, G_F, EXPS, BEXPS, MASK, SCALE, BSCALE = 4, 6, 8, 12, 16, 20, 21
PBIAS = 22
NBIAS = PBIAS + NBITS * DT
NVEC = NBIAS + NBITS * DT

def stages(text):
    return [(word[0], int(word[1:])) for word in text.split()]


L0_ORDER = stages("""
    R0 m0 G0 a0 G1 G2 G3 K0 G4 G5 W0 m1 K1 G6 Q0 G7 G8 A0 S0 T0 G9 a1 K2 K3 W1 P0 Q1 C0 d0 S1 T1 G10 P1 G11 G12
    W2 Q2 G13 K4 A1 B0 m2 G14 D0 S2 T2 a2 C1 Q3 A2 m3 d1 G15 W3 P2 C2 a3 D1 S3 T3 B1 E0 f0 A3 P3 d2 F0 B2 C3 d3
    D2 E1 D3 f1 B3 E2 F1 f2 E3 F2 f3 F3""")
ACT_ORDER = stages("""
    K0 K1 R0 Q0 a0 A0 G0 K2 S0 T0 P0 G1 G2 Q1 K3 a1 G3 G4 K4 W0 S1 T1 P1 G5 Q2 A1 d0 G6 G7 S2 T2 G8 G9 W1 D0 G10
    a2 G11 Q3 A2 P2 G12 W2 G13 G14 G15 W3 d1 D1 S3 T3 a3 A3 P3 f0 F0 d2 D2 d3 D3 f1 F1 f2 F2 f3 F3""")
DVE_ORDER = stages("""
    K0 K1 m0 Q0 R0 a0 m1 A0 S0 T0 P0 G0 a1 G1 Q1 G2 C0 G3 S1 T1 d0 m2 G4 P1 A1 Q2 G5 S2 T2 G6 a2 G7 C1 G8 D0 G9
    m3 A2 G10 d1 G11 P2 G12 a3 G13 Q3 G14 G15 C2 S3 T3 D1 E0 A3 f0 P3 F0 d2 C3 D2 d3 E1 D3 f1 E2 F1 f2 E3 f3 F2
    F3""")
POOL_ORDER = stages("""
    m0 m1 K2 G0 G1 G2 G3 K3 C0 W0 K4 G4 G5 m2 G6 G7 B0 G8 W1 G9 G10 C1 G11 m3 G12 W2 G13 G14 G15 W3 C2 B1 E0 C3
    B2 E1 B3 E2 E3""")
NBIT_CHUNKS = DT * NBITS


def numbered(kinds):
    found, n = {}, 0
    for key in L0_ORDER:
        if key[0] in kinds:
            found[key] = n
            n += 1 if key[0] == "R" else NT
    return found, n


TURN, TURNS = numbered("ADFPR")
XN, XNS = numbered("adf")
MOMENTS, NMOMENTS = numbered("mCE")
NORMS = [key for key in L0_ORDER if key[0] in "adf"]
LAST_TURN = {this: TURN[last[0].upper(), last[1]] for last, this in zip(NORMS, NORMS[1:])}
WIDE, WIDES = numbered("CE")
PROB, PROBS = numbered("S")
HALVES = {"S": range(NT // 2), "T": range(NT // 2, NT)}
P_BANK = (1, 0, 1, 1)


def flamingo_kernel(nc, x, ctxT, vecs, w0, bits, w1, w_gu, w_dn, topk_idx, topk_w, out):
    x_tiles = x.rearrange("(b i p) d -> b p i d", b=B, p=P)
    out_tiles = out.rearrange("(b i p) d -> b p i d", b=B, p=P)

    with ExitStack() as ctx:
        def sb(name, shape, dt=F32):
            return ctx.enter_context(nc.sbuf_tensor(name, shape, dt))

        def sem(name):
            return ctx.enter_context(nc.semaphore(name))

        def hi_lo(name, shape):
            return [sb(f"{name}_{part}", shape, F32R) for part in ("hi", "lo")]

        def f32(ap):
            return ap.bitcast(F32)

        x_sb = sb("x_sb", [P, B, NT, D])
        xnT = hi_lo("xnT", [P, B, DT, S])
        cT = hi_lo("cT", [P, B, CT, S])
        probT = hi_lo("probT", [P, NT, S])
        kv = hi_lo("kv", [P, 2, 2, S])
        qT = hi_lo("qT", [P, 2, S])
        oT = hi_lo("oT", [P, S])
        with nc.sbuf_tensor("planes", [P, 4, 2, D], F32) as planes:
            pass
        wq = hi_lo("wq", [P, DT * HD])
        wkv = hi_lo("wkv", [P, CT, 2 * HD])
        wo = hi_lo("wo", [P, D])
        sqs = hi_lo("sqs", [P, S])
        prob = sb("prob", [P, NT, S])
        xn = sb("xn", [P, NT, D])
        stage = sb("stage", [P, 4, S])
        kv_raw = sb("kv_raw", [P, NT, 2 * HD])
        ident = sb("ident", [P, P])
        vec = sb("vec", [P, NVEC])
        ones = sb("ones", [P, 2], F32R)
        minus_half = sb("minus_half", [P, NT])
        eps = sb("eps", [P, NT])
        tanh_g = sb("tanh_g", [P, 4])
        small = sb("small", [P, 16])
        bit_w = sb("bit_w", [P, NBITS])
        gain = sb("gain", [P, 1])
        stats = sb("stats", [P, 4, 6])
        mean_var = sb("mean_var", [P, B, NT, 2])
        var_eps = sb("var_eps", [P, NT])
        rstd = sb("rstd", [P, B, NT])
        ln_shift = sb("ln_shift", [P, B, NT])
        neg_max = sb("neg_max", [P, 2, NT])
        neg_bias = sb("neg_bias", [P, 2, NT])
        row_sum = sb("row_sum", [P, 2, NT])
        inv_sum = sb("inv_sum", [P, 2, NT])
        q_ss = sb("q_ss", [P, 2, NT])
        q_scale = sb("q_scale", [P, 2, NT])
        k_ss = sb("k_ss", [P, NT])
        k_ms = sb("k_ms", [P, NT])
        k_rs = sb("k_rs", [P, NT])
        idx = sb("idx", [P, NT, TOPK], I32)
        idx_f = sb("idx_f", [P, NT, TOPK])
        topw = sb("topw", [P, NT, TOPK])
        picked = sb("picked", [P, NT, TOPK])
        share = sb("share", [P, NT, E])

        sq = xn[:, 0, :]
        ksq = xn[:, 1, :].rearrange("p (i c) -> p i c", i=NT)
        bias_t = kv_raw[:, 0:2, :].rearrange("p a c -> p (a c)")
        bias_col = sb("bias_col", [P, (NBITS + 2) * DT])
        bit_acc = kv_raw[:, 2:4, :].rearrange("p a c -> p (a c)")
        w0s = oT
        split_stage = [bias_t, stage[:, 0:2, :], stage[:, 2:4, :], x_sb[:, B - 1, 0:2, :], x_sb[:, B - 1, 2:4, :]]
        wf = [t[:, :, :, :].rearrange("p a b c -> p (a b) c") for t in kv]

        s_bank = [ctx.enter_context(nc.psum_tensor(f"s_bank{i}", [P, 512], F32)) for i in range(2)]
        t_bank = [ctx.enter_context(nc.psum_tensor(f"t_bank{i}", [P, 512], F32)) for i in range(2)]
        w_bank = [ctx.enter_context(nc.psum_tensor(f"w_bank{i}", [P, 512], F32)) for i in range(2)]
        j_bank = [ctx.enter_context(nc.psum_tensor(f"j_bank{i}", [P, 512], F32)) for i in range(2)]

        def turn_bank(n):
            return (t_bank + j_bank)[n % 4] if n < TURNS else t_bank[(n - TURNS) % 2]

        vec_in, idx_in = sem("vec_in"), sem("idx_in")
        x_in = [sem(f"x_in{b}") for b in range(B)]
        split_in = [sem(f"split_in{i}") for i in range(1 + B)]
        planes_in = [sem(f"planes_in{i}") for i in range(4)]
        wq_in, wkv_in, wo_in = sem("wq_in"), sem("wkv_in"), sem("wo_in")
        gu_in, dn_in, stored, gate_in, up_in = sem("gu_in"), sem("dn_in"), sem("stored"), sem("gate_in"), sem("up_in")
        ident_ready, const_ready, gain_ready = sem("ident_ready"), sem("const_ready"), sem("gain_ready")
        gates_tanh, mask_tanh, bit_w_ready, share_ready = (
            sem("gates_tanh"), sem("mask_tanh"), sem("bit_w_ready"), sem("share_ready"))
        dve_own, pool_own = sem("dve_own"), sem("pool_own")
        stats_ready, shift_ready = sem("stats_ready"), sem("shift_ready")
        split_hi, split_lo = sem("split_hi"), sem("split_lo")
        bit_tanh, bit_diff, bit_added = sem("bit_tanh"), sem("bit_diff"), sem("bit_added")
        wf_hi, wf_lo, bias_spread = sem("wf_hi"), sem("wf_lo"), sem("bias_spread")
        moments, var_ready, rstd_ready, xn_ready, turned, turned_hi, turned_lo = (
            sem("moments"), sem("var_ready"), sem("rstd_ready"), sem("xn_ready"), sem("turned"), sem("turned_hi"), sem("turned_lo"))
        qk0_mm, qk0_hi, qk0_lo, e0_mm, e0_max, e0_exp, e0_inv, e0_scaled = (
            sem("qk0_mm"), sem("qk0_hi"), sem("qk0_lo"), sem("e0_mm"), sem("e0_max"), sem("e0_exp"), sem("e0_inv"),
            sem("e0_scaled"))
        wide_mm, wide_added, bias_added = sem("wide_mm"), sem("wide_added"), sem("bias_added")
        wq_hi, wq_lo, wkv_hi, wkv_lo, wo_hi, wo_lo = (
            sem("wq_hi"), sem("wq_lo"), sem("wkv_hi"), sem("wkv_lo"), sem("wo_hi"), sem("wo_lo"))
        kv_mm, kv_copied, k_squares, k_scaled, v_hi, v_lo = (
            sem("kv_mm"), sem("kv_copied"), sem("k_squares"), sem("k_scaled"), sem("v_hi"), sem("v_lo"))
        kT_mm, kT_hi, kT_lo = sem("kT_mm"), sem("kT_hi"), sem("kT_lo")
        q_mm, q_hi, q_lo, q_squared, sq_lo, q_ss_mm, q_ss_out, q_scale_ready = (
            sem("q_mm"), sem("q_hi"), sem("q_lo"), sem("q_squared"), sem("sq_lo"), sem("q_ss_mm"), sem("q_ss_out"),
            sem("q_scale_ready"))
        s_mm, s_max, p_exp, p_turned, p_hi, p_lo = (
            sem("s_mm"), sem("s_max"), sem("p_exp"), sem("p_turned"), sem("p_hi"), sem("p_lo"))
        pv_mm, o_hi, o_lo, w_mm, w_added = sem("pv_mm"), sem("o_hi"), sem("o_lo"), sem("w_mm"), sem("w_added")
        gate_hi = sem("gate_hi")
        gu_hi, gu_lo, dn_hi, dn_lo = sem("gu_hi"), sem("gu_lo"), sem("dn_hi"), sem("dn_lo")
        g_mm, u_mm, silu_ready, h_ready, h_hi, h_lo, d_mm, y_added = (
            sem("g_mm"), sem("u_mm"), sem("silu_ready"), sem("h_ready"), sem("h_hi"), sem("h_lo"), sem("d_mm"),
            sem("y_added"))

        def wait(eng, s, value):
            if isinstance(value, int) and value <= 0:
                return
            eng.wait_ge(s, value)

        def need(eng, s, per, h, k, c):
            wait(eng, s, h * (B * per) + (per * k + c))

        def need_e(eng, s, per, it, k, c):
            wait(eng, s, it * (2 * per) + (per * k + c))

        GU = 2 * DT * I
        DN = IT * D
        w_area = [t[:, 1:B, :, :].rearrange("p b j s -> p (b j s)") for t in xnT]
        c_area = [t[:, :, :, :].rearrange("p b j s -> p (b j s)") for t in cT]
        gu_w = [[w_area[part][:, slot * GU:(slot + 1) * GU] for part in range(2)] for slot in range(2)]
        dn_w = [[c_area[part][:, slot * DN:(slot + 1) * DN] for part in range(2)] for slot in range(2)]
        x_area = x_sb[:, 1:B, :, :].rearrange("p b i d -> p (b i d)")
        gu_stage, dn_stage = x_area[:, 0:GU], x_area[:, GU:GU + DN]
        first_gate = stage[:, :, :].rearrange("p a s -> p (a s)")[:, 0:DT * I]
        first_up = x_area[:, 0:DT * I]
        hT = [[t[:, 0:IT, :] for t in probT],
              [t[:, :, :, :].rearrange("p a b s -> p (a b) s")[:, 0:IT, :] for t in kv]]

        def cols(area, which, dj, j):
            at = (which * DT + dj) * I + j * P
            return area[:, at:at + IW[j]]

        block = ctx.enter_context(nc.Block())

        @block.sync
        def _(sp):
            def context(b):
                sp.dma_start(split_stage[1 + b], ctxT[b].rearrange("j p s -> p j s")).then_inc(split_in[1 + b], 16)

            def rows(b):
                sp.dma_start(x_sb[:, b, :, :], x_tiles[b]).then_inc(x_in[b], 16)

            def bit_planes(g):
                wait(sp, bit_tanh, g - 3)
                sp.dma_start(planes[:, g % 4, :, :], bits[g].rearrange("w p s -> p w s")).then_inc(
                    planes_in[g % 4], 16)

            sp.dma_start(split_stage[0], w0).then_inc(split_in[0], 16)
            context(0)
            sp.dma_start(vec[:], vecs).then_inc(vec_in, 16)
            rows(0)
            context(1)
            rows(1)
            for g in range(NBIT_CHUNKS):
                bit_planes(g)
                if g == 0:
                    context(2)
                    context(3)
                if g == 2:
                    rows(2)
                if g == 6:
                    sp.wait_ge(split_lo, 1 + B)
                    rows(3)
            sp.dma_start(idx[:], topk_idx).then_inc(idx_in, 16)
            sp.dma_start(topw[:], topk_w).then_inc(idx_in, 16)

            def head_weights(h):
                for n, (arrived, used) in enumerate(((wkv_in, wkv_lo), (wq_in, wq_lo), (wo_in, wo_lo))):
                    wait(sp, used, h)
                    src = w1[n, h] if isinstance(h, int) else w1[n, bass.ds(h, 1), :, :].rearrange("a p s -> p (a s)")
                    sp.dma_start(stage[:, n, :], src).then_inc(arrived, 16)

            sp.wait_ge(bit_added, NBIT_CHUNKS)
            head_weights(0)
            with sp.Fori(1, H) as h:
                head_weights(h)

            def store(b):
                sp.wait_ge(w_added, 4 * (B * (H - 1) + b + 1))
                sp.dma_start(out_tiles[b], x_sb[:, b, :, :]).then_inc(stored, 16)

            sp.wait_ge(wo_lo, H)
            sp.wait_ge(wq_lo, H)
            sp.dma_start(first_gate, w_gu[0, :, 0:DT * I]).then_inc(gate_in, 16)
            store(1)
            sp.wait_ge(stored, 16)
            sp.dma_start(first_up, w_gu[0, :, DT * I:]).then_inc(up_in, 16)
            store(2)
            store(3)
            sp.wait_ge(stored, 16 * (B - 1))

            sp.dma_start(dn_stage, w_dn[0]).then_inc(dn_in, 16)
            with sp.Fori(1, E) as e:
                for area, w, arrived, used in ((gu_stage, w_gu, gu_in, (gu_lo, 2)), (dn_stage, w_dn, dn_in, (dn_lo, 1))):
                    wait(sp, used[0], used[1] * e)
                    sp.dma_start(area, w[bass.ds(e, 1), :, :].rearrange("a p s -> p (a s)")).then_inc(arrived, 16)
            for t in range(NT):
                sp.wait_ge(y_added, NT * (E - 1) + t + 1)
                sp.dma_start(out_tiles[0][:, t, :], x_sb[:, 0, t, :]).then_inc(stored, 16)
            sp.wait_ge(stored, 16 * (B - 1 + NT))

        @block.tensor
        def _(pe):
            def product(dst, left, right, first=True, last=True):
                (lh, ll), (rh, rl) = left, right
                pe.matmul(dst, lh, rl, start=first, stop=False)
                pe.matmul(dst, lh, rh, start=False, stop=False)
                return pe.matmul(dst, ll, rh, start=False, stop=last)

            def turn(n, tile, ready, count):
                pe.wait_ge(ready, count)
                if n < TURNS:
                    wait(pe, turned_lo, n - 3)
                elif n < TURNS + 2:
                    pe.wait_ge(p_lo, 4 * B * H)
                else:
                    pe.wait_ge(turned_lo, n - 1)
                for j in range(4):
                    last = pe.transpose(turn_bank(n)[:, j * P:(j + 1) * P], tile[:, j * P:(j + 1) * P], ident[:])
                last.then_inc(turned, 1)

            pe.wait_ge(ident_ready, 2)
            for kind, b in L0_ORDER:
                if kind in "ADF":
                    for i in range(NT):
                        turn(TURN[kind, b] + i, xn[:, i, :], xn_ready, XN[kind.lower(), b] + i + 1)
                elif kind == "P":
                    for i in range(NT):
                        turn(TURN[kind, b] + i, prob[:, i, :], e0_scaled, PROB["S", b] + i + 1)
                elif kind == "R":
                    turn(TURN[kind, b], bit_acc, bias_spread, 1)
                elif kind == "Q":
                    pe.wait_ge(split_lo, 2 + b)
                    wait(pe, e0_exp, NT * b)
                    for n in range(2):
                        for cj in range(CT):
                            at = (n * CT + cj) * P
                            last = product(s_bank[n][:], [t[:, at:at + P] for t in w0s],
                                           [t[:, b, cj, :] for t in cT], cj == 0, cj == CT - 1)
                        last.then_inc(qk0_mm, 1)
                elif kind in HALVES:
                    pe.wait_ge(qk0_lo, 2 * (b + 1))
                    for i in HALVES[kind]:
                        wait(pe, e0_exp, PROB["S", b] + i - 1)
                        product(s_bank[i % 2][:], [t[:, 0, i * P:(i + 1) * P] for t in qT],
                                [t[:, 1, :] for t in qT]).then_inc(e0_mm, 1)
                elif kind in "CE":
                    pe.wait_ge(turned_lo, NT + (max(TURN["A", b], TURN["P", b]) if kind == "C" else TURN["D", b]))
                    if kind == "E":
                        pe.wait_ge(wf_lo, DT)
                    for i in range(NT):
                        n = WIDE[kind, b] + i
                        wait(pe, wide_added, n - 1)
                        right = probT if kind == "C" else wf
                        for j in range(DT):
                            last = product(w_bank[n % 2][:], [t[:, b, j, i * P:(i + 1) * P] for t in xnT],
                                           [t[:, j, :] for t in right], j == 0, j == DT - 1)
                        last.then_inc(wide_mm, 1)

            def step(h, k, proj=True, score=True, value=True):
                def scores(i):
                    if not score:
                        return
                    u = k - 1
                    if i == 0:
                        need(pe, q_lo, 1, h, u, 1)
                        need(pe, kT_lo, 1, h, u, 1)
                    need(pe, p_exp, 4, h, u, i - 1)
                    product(s_bank[i % 2][:], [t[:, u % 2, i * P:(i + 1) * P] for t in qT],
                            [t[:, u % 2, 0, :] for t in kv]).then_inc(s_mm, 1)

                def probs(i):
                    if not score:
                        return
                    u = k - 1
                    need(pe, p_exp, 4, h, u, i + 1)
                    if i == 1:
                        need(pe, q_ss_out, 1, h, u, 1)
                    else:
                        need(pe, p_lo, 4, h, u, (0, None, 1, 3)[i])
                    for j in range(4):
                        last = pe.transpose(t_bank[P_BANK[i]][:, j * P:(j + 1) * P], prob[:, i, j * P:(j + 1) * P],
                                            ident[:])
                    last.then_inc(p_turned, 1)

                def values():
                    if not value:
                        return
                    w = k - 2
                    need(pe, p_lo, 4, h, w, 4)
                    need(pe, v_lo, 1, h, w, 1)
                    need(pe, kv_copied, 2, h, k - 1, 2 if proj else 0)
                    for j in range(NT):
                        last = product(j_bank[0][:], [t[:, w % 2, 1, j * P:(j + 1) * P] for t in kv],
                                       [t[:, j, :] for t in probT], j == 0, j == NT - 1)
                    last.then_inc(pv_mm, 1)

                def project_out(i):
                    if not value:
                        return
                    w = k - 2
                    if i == 0:
                        need(pe, o_lo, 1, h, w, 1)
                        wait(pe, wo_lo, h + (1 if k >= 2 else 0))
                    need(pe, w_added, 4, h, w, i - 1)
                    product(w_bank[i % 2][:], [t[:, i * P:(i + 1) * P] for t in oT],
                            [t[:] for t in wo]).then_inc(w_mm, 1)

                def key_value(half):
                    if not proj:
                        return
                    if half == 0:
                        wait(pe, wkv_lo, h + 1)
                        need(pe, q_lo, 1, h, k - 1, 1)
                        need(pe, q_squared, 2, h, k - 1, 2)
                    else:
                        need(pe, kv_copied, 2, h, k - 1, 2)
                        if value:
                            need(pe, o_lo, 1, h, k - 2, 1)
                    for a in range(2):
                        t0 = (2 * half + a) * P
                        for cj in range(CT):
                            last = product(j_bank[1 - half][:, a * 2 * HD:(a + 1) * 2 * HD],
                                           [t[:, k, cj, t0:t0 + P] for t in cT],
                                           [t[:, cj, :] for t in wkv], cj == 0, cj == CT - 1)
                    last.then_inc(kv_mm, 1)

                def query(tiles):
                    if not proj:
                        return
                    if 0 in tiles:
                        wait(pe, wq_lo, h + 1)
                        need(pe, kv_copied, 2, h, k, 1)
                        if isinstance(h, int) and h == 0:
                            pe.wait_ge(turned_lo, TURN["F", k] + 4)
                    for dj in tiles:
                        last = product(j_bank[1][:], [t[:, dj * HD:(dj + 1) * HD] for t in wq],
                                       [t[:, k, dj, :] for t in xnT], dj == 0, dj == DT - 1)
                    if DT - 1 in tiles:
                        last.then_inc(q_mm, 1)

                def key_turn():
                    if not proj:
                        return
                    need(pe, k_scaled, 1, h, k, 1)
                    if score:
                        need(pe, p_lo, 4, h, k - 1, 2)
                    for j in range(NT):
                        last = pe.transpose(t_bank[0][:, j * P:(j + 1) * P], kv_raw[:, j, 0:HD], ident[:])
                    last.then_inc(kT_mm, 1)

                def query_squares():
                    if not score:
                        return
                    u = k - 1
                    need(pe, sq_lo, 1, h, u, 1)
                    need(pe, kT_lo, 1, h, u, 1)
                    for i in range(NT):
                        here = slice(i * P, (i + 1) * P)
                        pe.matmul(t_bank[0][:, 2 * i:2 * i + 2], sqs[0][:, here], ones[:], start=True, stop=False)
                        last = pe.matmul(t_bank[0][:, 2 * i:2 * i + 2], sqs[1][:, here], ones[:], start=False,
                                         stop=True)
                    last.then_inc(q_ss_mm, 1)

                scores(0)
                scores(1)
                query_squares()
                values()
                key_value(0)
                probs(0)
                scores(2)
                key_value(1)
                project_out(0)
                scores(3)
                probs(1)
                query((0, 1))
                probs(2)
                query((2, 3))
                project_out(1)
                key_turn()
                probs(3)
                project_out(2)
                project_out(3)

            pe.wait_ge(const_ready, 2)
            pe.wait_ge(turned_lo, TURNS)
            step(0, 0, score=False, value=False)
            step(0, 1, value=False)
            step(0, 2)
            step(0, 3)
            with pe.Fori(1, H) as h:
                for k in range(B):
                    step(h, k)
            step(H, 0, proj=False)
            for i in range(NT):
                turn(TURNS + i, xn[:, i, :], xn_ready, XNS + i + 1)
            step(H, 1, proj=False, score=False)

            def expert_step(it, k, up=True, down=True):
                def gate_up(j):
                    if not up:
                        return
                    bank = (3 * k + j) % 2
                    if j == 0:
                        need_e(pe, gu_lo, 2, it, k, 2)
                    need_e(pe, silu_ready, IT, it, k, j - 1)
                    for dj in range(DT):
                        last = product(s_bank[bank][0:IW[j], :], [cols(a, 0, dj, j) for a in gu_w[k % 2]],
                                       [t[:, 0, dj, :] for t in xnT], dj == 0, dj == DT - 1)
                    last.then_inc(g_mm, 1)
                    need_e(pe, h_ready, IT, it, k, j - 1)
                    for dj in range(DT):
                        last = product(t_bank[bank][0:IW[j], :], [cols(a, 1, dj, j) for a in gu_w[k % 2]],
                                       [t[:, 0, dj, :] for t in xnT], dj == 0, dj == DT - 1)
                    last.then_inc(u_mm, 1)

                def project_down(t):
                    if not down:
                        return
                    e = k - 1
                    if t == 0:
                        need_e(pe, h_hi, IT, it, e, IT)
                        need_e(pe, h_lo, IT, it, e, IT)
                        need_e(pe, dn_lo, 1, it, e, 1)
                    need_e(pe, y_added, NT, it, e, t - 1)
                    for j in range(IT):
                        last = product(w_bank[t % 2][:], [a[0:IW[j], j, t * P:(t + 1) * P] for a in hT[e % 2]],
                                       [a[0:IW[j], j * D:(j + 1) * D] for a in dn_w[e % 2]], j == 0, j == IT - 1)
                    last.then_inc(d_mm, 1)

                gate_up(0)
                project_down(0)
                project_down(1)
                gate_up(1)
                project_down(2)
                gate_up(2)
                project_down(3)

            pe.wait_ge(turned_lo, TURNS + NT)
            expert_step(0, 0, down=False)
            expert_step(0, 1)
            with pe.Fori(1, E // 2) as it:
                expert_step(it, 0)
                expert_step(it, 1)
            expert_step(E // 2, 0, up=False)

        @block.scalar
        def _(act):
            def copy_hi(dst, src):
                return nc.scalar.copy(dst, src)

            def turned_tile(kind, b, i, n):
                act.wait_ge(turned, n + 1)
                dst = probT[0][:, :, i * P:(i + 1) * P] if kind == "P" else xnT[0][:, b, :, i * P:(i + 1) * P]
                copy_hi(dst, turn_bank(n)[:].rearrange("p (j q) -> p j q", j=4)).then_inc(turned_hi, 1)

            act.wait_ge(vec_in, 16)
            nc.scalar.activation(tanh_g[:], vec[:, G_X:G_X + 4], ACT.Tanh).then_inc(gates_tanh, 1)
            nc.scalar.activation(small[:, 0:NBITS], vec[:, MASK:MASK + NBITS], ACT.Tanh, scale=0.5).then_inc(
                mask_tanh, 1)
            for kind, b in ACT_ORDER:
                if kind == "K":
                    act.wait_ge(split_in[b], 16)
                    copy_hi(w0s[0][:] if b == 0 else cT[0][:, b - 1, :, :], split_stage[b]).then_inc(split_hi, 1)
                elif kind in "ADF":
                    for i in range(NT):
                        turned_tile(kind, b, i, TURN[kind, b] + i)
                elif kind == "Q":
                    for n, bias in enumerate((BQ, BK)):
                        act.wait_ge(qk0_mm, 2 * b + n + 1)
                        wait(act, e0_mm, 4 * b)
                        nc.scalar.activation(qT[0][:, n, :], s_bank[n][:], ACT.Identity,
                                             bias=vec[:, bias:bias + 1]).then_inc(qk0_hi, 1)
                elif kind in HALVES:
                    def scaled(i):
                        act.wait_ge(e0_inv, PROB["S", b] + i + 1)
                        nc.scalar.mul(prob[:, i, :], prob[:, i, :], inv_sum[:, b % 2, i:i + 1]).then_inc(e0_scaled, 1)

                    for i in HALVES[kind]:
                        n = PROB["S", b] + i
                        act.wait_ge(e0_max, n + 1)
                        if b:
                            act.wait_ge(turned, TURN["P", b - 1] + i + 1)
                        nc.scalar.activation(prob[:, i, :], s_bank[i % 2][:], ACT.Exp, bias=neg_max[:, b % 2, i:i + 1],
                                             accum_out=row_sum[:, b % 2, i:i + 1]).then_inc(e0_exp, 1)
                        if i:
                            scaled(i - 1)
                        if i == NT - 1:
                            scaled(i)
                elif kind == "P":
                    for i in range(NT):
                        turned_tile(kind, b, i, TURN[kind, b] + i)
                elif kind == "R":
                    act.wait_ge(turned, TURN[kind, b] + 1)
                    act.wait_ge(split_lo, 1)
                    nc.scalar.copy(bias_t[:, 0:D // 2], turn_bank(TURN[kind, b])[:, 0:D // 2]).then_inc(turned_hi, 1)
                elif kind == "G":
                    act.wait_ge(planes_in[b % 4], 16 * (b // 4 + 1))
                    if b < 2:
                        act.wait_ge(split_lo, 2 + b)
                    else:
                        act.wait_ge(bit_added, b - 1)
                    at = 2 * (b % 2)
                    nc.scalar.activation(stage[:, at:at + 2, :], planes[:, b % 4, :, :], ACT.Tanh,
                                         scale=0.5).then_inc(bit_tanh, 1)
                elif kind == "W":
                    act.wait_ge(bit_added, NBITS * (b + 1))
                    copy_hi(wf[0][:, b, :], bit_acc).then_inc(wf_hi, 1)
                elif kind in "adf":
                    act.wait_ge(shift_ready, XN[kind, b] // NT + 1)
                    for i in range(NT):
                        if XN[kind, b]:
                            act.wait_ge(turned, LAST_TURN[kind, b] + i + 1)
                        nc.scalar.activation(xn[:, i, :], x_sb[:, b, i, :], ACT.Identity, bias=ln_shift[:, b, i:i + 1],
                                             scale=rstd[:, b, i:i + 1]).then_inc(xn_ready, 1)

            def step(h, k, proj=True, score=True, value=True):
                def softmax(i):
                    if not score:
                        return
                    u = k - 1
                    need(act, s_max, 4, h, u, i + 1)
                    need(act, p_turned, 4, h, u - 1, i + 1)
                    nc.scalar.activation(prob[:, i, :], s_bank[i % 2][:], ACT.Exp,
                                         bias=neg_bias[:, u % 2, i:i + 1], scale=q_scale[:, u % 2, i:i + 1],
                                         accum_out=row_sum[:, u % 2, i:i + 1]).then_inc(p_exp, 1)

                def probs_hi(i):
                    if not score:
                        return
                    need(act, p_turned, 4, h, k - 1, i + 1)
                    copy_hi(probT[0][:, :, i * P:(i + 1) * P],
                            t_bank[P_BANK[i]][:].rearrange("p (j q) -> p j q", j=4)).then_inc(p_hi, 1)

                def key_value_rows(half):
                    if not proj:
                        return
                    need(act, kv_mm, 2, h, k, half + 1)
                    if half == 0:
                        need(act, kT_mm, 1, h, k - 1, 1)
                        need(act, v_lo, 1, h, k - 1, 1)
                    nc.scalar.copy(kv_raw[:, 2 * half:2 * half + 2, :],
                                   j_bank[1 - half][:].rearrange("p (a c) -> p a c", a=2)).then_inc(kv_copied, 1)

                if k == 0 and proj:
                    wait(act, wkv_in, h * 16 + 16)
                    need(act, kv_mm, 2, h, -1, 2)
                    copy_hi(wkv[0][:, :, :].rearrange("p a c -> p (a c)"), stage[:, 0, :]).then_inc(wkv_hi, 1)
                if k == 2:
                    wait(act, wo_in, h * 16 + 16)
                    need(act, w_mm, 4, h, -1, 4)
                    copy_hi(wo[0][:], stage[:, 2, :]).then_inc(wo_hi, 1)
                softmax(0)
                if k == 0 and proj:
                    wait(act, wq_in, h * 16 + 16)
                    need(act, q_mm, 1, h, -1, 1)
                    copy_hi(wq[0][:], stage[:, 1, :]).then_inc(wq_hi, 1)
                if value:
                    need(act, pv_mm, 1, h, k - 2, 1)
                    need(act, w_mm, 4, h, k - 3, 4)
                    copy_hi(oT[0][:], j_bank[0][:]).then_inc(o_hi, 1)
                softmax(1)
                key_value_rows(0)
                probs_hi(0)
                key_value_rows(1)
                if proj:
                    need(act, kv_copied, 2, h, k, 2)
                    need(act, k_scaled, 1, h, k - 1, 1)
                    for i in range(NT):
                        nc.scalar.activation(ksq[:, i, :], kv_raw[:, i, 0:HD], ACT.Square, scale=HD ** -0.5,
                                             accum_out=k_ss[:, i:i + 1]).then_inc(k_squares, 1)
                softmax(2)
                softmax(3)
                probs_hi(1)
                probs_hi(2)
                if proj:
                    need(act, q_mm, 1, h, k, 1)
                    need(act, s_mm, 4, h, k - 2, 4)
                    copy_hi(qT[0][:, k % 2, :], j_bank[1][:]).then_inc(q_hi, 1)
                    need(act, kT_mm, 1, h, k, 1)
                    nc.scalar.activation(kv[0][:, k % 2, 0, :], t_bank[0][:], ACT.Copy,
                                         scale=gain[:]).then_inc(kT_hi, 1)
                    need(act, q_lo, 1, h, k, 1)
                    need(act, q_ss_mm, 1, h, k - 1, 1)
                    nc.scalar.activation(sqs[0][:], j_bank[1][:], ACT.Square).then_inc(q_squared, 1)
                    need(act, sq_lo, 1, h, k - 1, 1)
                    nc.scalar.activation(sq[:], j_bank[1][:], ACT.Square).then_inc(q_squared, 1)
                probs_hi(3)

            act.wait_ge(gain_ready, 1)
            step(0, 0, score=False, value=False)
            step(0, 1, value=False)
            step(0, 2)
            step(0, 3)
            with act.Fori(1, H) as h:
                for k in range(B):
                    step(h, k)
            act.wait_ge(q_mm, B * (H - 1) + 3)
            act.wait_ge(gate_in, 16)
            copy_hi(gu_w[0][0][:, 0:DT * I], first_gate).then_inc(gate_hi, 1)
            step(H, 0, proj=False)
            for i in range(NT):
                turned_tile("M", 0, i, TURNS + i)
            act.wait_ge(up_in, 16)
            copy_hi(gu_w[0][0][:, DT * I:], first_up).then_inc(gu_hi, 1)
            step(H, 1, proj=False, score=False)

            def gate_up_hi(it, k):
                need_e(act, gu_in, 16, it, k, 0)
                need_e(act, u_mm, IT, it, k - 2, IT)
                copy_hi(gu_w[k % 2][0], gu_stage).then_inc(gu_hi, 1)

            def expert_step(it, k, more=True):
                def silu(j):
                    need_e(act, g_mm, IT, it, k, j + 1)
                    need_e(act, h_ready, IT, it, k, j - 1)
                    g = (IT * k + j) % 2
                    nc.scalar.activation(prob[0:IW[j], g, :], s_bank[g][0:IW[j], :], ACT.Silu).then_inc(silu_ready, 1)

                def inner_hi(j):
                    need_e(act, h_ready, IT, it, k, j + 1)
                    if j == 0:
                        need_e(act, d_mm, NT, it, k - 2, NT)
                    copy_hi(hT[k % 2][0][0:IW[j], j, :],
                            prob[0:IW[j], 2 + (IT * k + j) % 2, :]).then_inc(h_hi, 1)

                silu(0)
                need_e(act, dn_in, 16, it, k, 16)
                need_e(act, d_mm, NT, it, k - 2, NT)
                copy_hi(dn_w[k % 2][0], dn_stage).then_inc(dn_hi, 1)
                inner_hi(0)
                silu(1)
                if more:
                    gate_up_hi(it, k + 1)
                inner_hi(1)
                silu(2)
                inner_hi(2)

            act.wait_ge(q_mm, B * H)
            act.wait_ge(kv_mm, 2 * B * H)
            expert_step(0, 0)
            expert_step(0, 1)
            with act.Fori(1, E // 2 - 1) as it:
                expert_step(it, 0)
                expert_step(it, 1)
            expert_step(E // 2 - 1, 0)
            expert_step(E // 2 - 1, 1, more=False)

        @block.vector
        def _(dve):
            done = [0]

            def then_wait(ins):
                done[0] += 1
                ins.then_inc(dve_own, 1)
                dve.wait_ge(dve_own, done[0])

            def lower(dst, src, hi):
                return nc.vector.tensor_tensor(dst, src, hi, ALU.subtract)

            def statistics(b, i, n):
                wait(dve, moments, n - 3)
                nc.vector.bn_stats(stats[:, n % 4, :], x_sb[:, b, i, :]).then_inc(stats_ready, 1)

            def mean_variance(b, i, n):
                dve.wait_ge(stats_ready, n + 1)
                nc.vector.bn_aggr(mean_var[:, b, i, :], stats[:, n % 4, :]).then_inc(moments, 1)

            def batch_moments(b, first):
                for i in range(NT):
                    statistics(b, i, first + i)
                for i in range(NT):
                    mean_variance(b, i, first + i)

            def turned_tile(kind, b, i, n):
                dve.wait_ge(turned_hi, n + 1)
                where = [t[:, :, i * P:(i + 1) * P] if kind == "P" else t[:, b, :, i * P:(i + 1) * P]
                         for t in (probT if kind == "P" else xnT)]
                lower(where[1], turn_bank(n)[:].rearrange("p (j q) -> p j q", j=4), f32(where[0])).then_inc(
                    turned_lo, 1)

            nc.vector.memset(f32(ones[:]), 1.0).then_inc(const_ready, 1)
            nc.vector.memset(minus_half[:], -0.5).then_inc(const_ready, 1)
            nc.vector.memset(eps[:], EPS).then_inc(const_ready, 1)
            dve.wait_ge(vec_in, 16)
            nc.vector.tensor_tensor(gain[:], vec[:, GQ:GQ + 1], vec[:, GK:GK + 1], ALU.mult).then_inc(gain_ready, 1)
            dve.wait_ge(gates_tanh, 1)
            dve.wait_ge(mask_tanh, 1)
            then_wait(nc.vector.tensor_scalar(small[:, 4:8], small[:, 0:4], 0.5, 0.5, ALU.mult, ALU.add))
            then_wait(nc.vector.tensor_tensor(small[:, 0:4], small[:, 4:8], vec[:, EXPS:EXPS + NBITS], ALU.mult))
            then_wait(nc.vector.tensor_scalar(small[:, 4:8], small[:, 0:4], vec[:, SCALE:SCALE + 1],
                                              tanh_g[:, 2:3], ALU.mult, ALU.mult))
            then_wait(nc.vector.tensor_scalar(bit_w[:], small[:, 4:8], 0.5, None, ALU.mult))

            bias_sum = bias_col[:, NBITS * DT:(NBITS + 1) * DT]
            bias = bias_col[:, (NBITS + 1) * DT:]
            steps = float(2 ** NBITS - 1)
            then_wait(nc.vector.tensor_tensor(bias_col[:, 0:NBITS * DT], vec[:, PBIAS:PBIAS + NBITS * DT],
                                              vec[:, NBIAS:NBIAS + NBITS * DT], ALU.subtract))
            then_wait(nc.vector.tensor_scalar(bias_sum, bias_col[:, 0:DT], vec[:, BEXPS:BEXPS + 1], None, ALU.mult))
            for n in range(1, NBITS):
                then_wait(nc.vector.scalar_tensor_tensor(
                    out=bias_sum, in0=bias_col[:, n * DT:(n + 1) * DT], scalar=vec[:, BEXPS + n:BEXPS + n + 1],
                    in1=bias_sum, op0=ALU.mult, op1=ALU.add))
            then_wait(nc.vector.tensor_scalar(bias, bias_sum, -1.0, 1.0, ALU.max, ALU.min))
            then_wait(nc.vector.tensor_scalar(bias, bias, steps, None, ALU.mult))
            then_wait(nc.vector.tensor_scalar(bias, bias, ROUND, None, ALU.add))
            then_wait(nc.vector.tensor_scalar(bias, bias, -ROUND, 1.0 / steps, ALU.add, ALU.mult))
            then_wait(nc.vector.tensor_scalar(bias, bias, vec[:, BSCALE:BSCALE + 1], tanh_g[:, 2:3],
                                              ALU.mult, ALU.mult))
            nc.vector.tensor_copy(bit_acc.rearrange("p (j q) -> p j q", j=DT),
                                  bias.unsqueeze(2).to_broadcast([P, DT, P])).then_inc(bias_spread, 1)

            for kind, b in DVE_ORDER:
                if kind in "ADF":
                    for i in range(NT):
                        turned_tile(kind, b, i, TURN[kind, b] + i)
                elif kind == "m":
                    dve.wait_ge(x_in[b], 16)
                    batch_moments(b, MOMENTS[kind, b])
                elif kind in "adf":
                    of = {"a": "m", "d": "C", "f": "E"}[kind]
                    dve.wait_ge(rstd_ready, MOMENTS[of, b] // NT + 1)
                    nc.vector.scalar_tensor_tensor(out=ln_shift[:, b, :], in0=mean_var[:, b, :, 0], scalar=-1.0,
                                                   in1=rstd[:, b, :], op0=ALU.mult, op1=ALU.mult).then_inc(
                                                       shift_ready, 1)
                elif kind == "R":
                    dve.wait_ge(turned_hi, TURN[kind, b] + 1)
                    nc.vector.tensor_copy(bias_t[:, D // 2:], turn_bank(TURN[kind, b])[:, D // 2:]).then_inc(
                        turned_lo, 1)
                elif kind == "K" and b < 2:
                    dve.wait_ge(split_hi, b + 1)
                    hi, lo = [t[:] if b == 0 else t[:, b - 1, :, :] for t in (w0s if b == 0 else cT)]
                    lower(lo, split_stage[b], f32(hi)).then_inc(split_lo, 1)
                elif kind == "Q":
                    for n, bias in enumerate((BQ, BK)):
                        dve.wait_ge(qk0_hi, 2 * b + n + 1)
                        nc.vector.scalar_tensor_tensor(
                            out=qT[1][:, n, :], in0=s_bank[n][:], scalar=vec[:, bias:bias + 1],
                            in1=f32(qT[0][:, n, :]), op0=ALU.add, op1=ALU.subtract).then_inc(qk0_lo, 1)
                elif kind in HALVES:
                    def inverse(i):
                        dve.wait_ge(e0_exp, PROB["S", b] + i + 1)
                        nc.vector.reciprocal(inv_sum[:, b % 2, i:i + 1], row_sum[:, b % 2, i:i + 1]).then_inc(
                            e0_inv, 1)
                    for i in HALVES[kind]:
                        dve.wait_ge(e0_mm, PROB["S", b] + i + 1)
                        nc.vector.tensor_reduce(neg_max[:, b % 2, i:i + 1], s_bank[i % 2][:], AX_X, ALU.max,
                                                negate=True).then_inc(e0_max, 1)
                        if i:
                            inverse(i - 1)
                        if i == NT - 1:
                            inverse(i)
                elif kind == "P":
                    for i in range(NT):
                        turned_tile(kind, b, i, TURN[kind, b] + i)
                elif kind in "CE":
                    def add(i):
                        n = WIDE[kind, b] + i
                        dve.wait_ge(wide_mm, n + 1)
                        here = x_sb[:, b, i, :]
                        if kind == "C":
                            nc.vector.scalar_tensor_tensor(
                                out=here, in0=w_bank[n % 2][:], scalar=tanh_g[:, 0:1], in1=here,
                                op0=ALU.mult, op1=ALU.add).then_inc(wide_added, 1)
                        else:
                            dve.wait_ge(bias_added, NT * b + i + 1)
                            nc.vector.tensor_tensor(here, w_bank[n % 2][:], here, ALU.add).then_inc(wide_added, 1)

                    for i in range(NT + 2):
                        if i < NT:
                            add(i)
                        if 0 < i <= NT:
                            dve.wait_ge(wide_added, WIDE[kind, b] + i)
                            statistics(b, i - 1, MOMENTS[kind, b] + i - 1)
                        if 1 < i:
                            mean_variance(b, i - 2, MOMENTS[kind, b] + i - 2)
                elif kind == "G":
                    j, n = divmod(b, NBITS)
                    dve.wait_ge(bit_diff, b + 1)
                    if b == 0:
                        dve.wait_ge(turned, TURN["R", 0] + 1)
                    if n == 0:
                        wait(dve, wf_lo, j)
                        nc.vector.tensor_scalar(bit_acc, stage[:, 2 * (b % 2), :], bit_w[:, n:n + 1], None,
                                                ALU.mult).then_inc(bit_added, 1)
                    else:
                        dve.wait_ge(bit_added, b)
                        nc.vector.scalar_tensor_tensor(out=bit_acc, in0=stage[:, 2 * (b % 2), :],
                                                       scalar=bit_w[:, n:n + 1], in1=bit_acc, op0=ALU.mult,
                                                       op1=ALU.add).then_inc(bit_added, 1)

            dve.wait_ge(idx_in, 32)
            then_wait(nc.vector.tensor_copy(idx_f[:], idx[:]))
            for e in range(E):
                then_wait(nc.vector.scalar_tensor_tensor(
                    out=picked[:], in0=idx_f[:], scalar=float(e), in1=topw[:], op0=ALU.is_equal, op1=ALU.mult))
                then_wait(nc.vector.tensor_reduce(share[:, :, e:e + 1], picked[:], AX_X, ALU.add))
            then_wait(nc.vector.tensor_scalar(share[:], share[:], tanh_g[:, 3:4], None, ALU.mult))

            own_max, own_inv = sem("own_max"), sem("own_inv")

            def step(h, k, proj=True, score=True, value=True, batch0_done=False):
                def maximum(i):
                    if not score:
                        return
                    u = k - 1
                    need(dve, s_mm, 4, h, u, i + 1)
                    nc.vector.tensor_reduce(neg_max[:, u % 2, i:i + 1], s_bank[i % 2][:], AX_X, ALU.max,
                                            negate=True).then_inc(own_max, 1)

                def shift(i):
                    if not score:
                        return
                    u = k - 1
                    if i == 0:
                        need(dve, q_scale_ready, 1, h, u, 1)
                    need(dve, own_max, 4, h, u, i + 1)
                    nc.vector.tensor_tensor(neg_bias[:, u % 2, i:i + 1], neg_max[:, u % 2, i:i + 1],
                                            q_scale[:, u % 2, i:i + 1], ALU.mult).then_inc(s_max, 1)

                def probs_lo(i):
                    if not score:
                        return
                    need(dve, p_hi, 4, h, k - 1, i + 1)
                    hi, lo = [t[:, :, i * P:(i + 1) * P] for t in probT]
                    lower(lo, t_bank[P_BANK[i]][:].rearrange("p (j q) -> p j q", j=4), f32(hi)).then_inc(p_lo, 1)

                def add(i):
                    if not value:
                        return
                    w = k - 2
                    need(dve, w_mm, 4, h, w, i + 1)
                    if i == 0:
                        need(dve, own_inv, 2, h, w, 2)
                    here = x_sb[:, w % B, i, :]
                    nc.vector.scalar_tensor_tensor(out=here, in0=w_bank[i % 2][:], scalar=inv_sum[:, w % 2, i:i + 1],
                                                   in1=here, op0=ALU.mult, op1=ALU.add).then_inc(w_added, 1)

                maximum(0)
                maximum(1)
                if score:
                    need(dve, q_ss_mm, 1, h, k - 1, 1)
                    nc.vector.tensor_scalar(q_ss[:, (k - 1) % 2, :], t_bank[0][:, 0:2 * NT:2], HD * EPS, None,
                                            ALU.add).then_inc(q_ss_out, 1)
                shift(0)
                shift(1)
                if value:
                    w = k - 2
                    nc.vector.reciprocal(inv_sum[:, w % 2, :], row_sum[:, w % 2, :]).then_inc(own_inv, 1)
                    need(dve, own_inv, 2, h, w, 1)
                    nc.vector.tensor_scalar(inv_sum[:, w % 2, :], inv_sum[:, w % 2, :], tanh_g[:, 1:2], None,
                                            ALU.mult).then_inc(own_inv, 1)
                    if batch0_done:
                        dve.wait_ge(w_added, 4 * (B * (H - 1) + 1))
                        batch_moments(0, NMOMENTS)
                    need(dve, o_hi, 1, h, w, 1)
                    lower(oT[1][:], j_bank[0][:], f32(oT[0][:])).then_inc(o_lo, 1)
                probs_lo(0)
                maximum(2)
                shift(2)
                if proj:
                    need(dve, kv_copied, 2, h, k, 2)
                    need(dve, pv_mm, 1, h, k - 2, 1)
                    nc.vector.tensor_copy(kv[0][:, k % 2, 1, :].rearrange("p (j c) -> p j c", j=NT),
                                          kv_raw[:, :, HD:2 * HD]).then_inc(v_hi, 1)
                add(0)
                maximum(3)
                shift(3)
                probs_lo(1)
                probs_lo(2)
                if proj:
                    need(dve, q_hi, 1, h, k, 1)
                    lower(qT[1][:, k % 2, :], j_bank[1][:], f32(qT[0][:, k % 2, :])).then_inc(q_lo, 1)
                add(1)
                if batch0_done:
                    dve.wait_ge(sq_lo, B * H)
                    dve.wait_ge(k_squares, 4 * B * H)
                    dve.wait_ge(rstd_ready, NMOMENTS // NT + 1)
                    for i in range(NT):
                        nc.vector.tensor_scalar(xn[:, i, :], x_sb[:, 0, i, :], mean_var[:, 0, i, 0:1],
                                                rstd[:, 0, i:i + 1], ALU.subtract, ALU.mult).then_inc(xn_ready, 1)
                if proj:
                    need(dve, kT_hi, 1, h, k, 1)
                    nc.vector.scalar_tensor_tensor(
                        out=kv[1][:, k % 2, 0, :], in0=t_bank[0][:], scalar=gain[:], in1=f32(kv[0][:, k % 2, 0, :]),
                        op0=ALU.mult, op1=ALU.subtract).then_inc(kT_lo, 1)
                probs_lo(3)
                add(2)
                add(3)

            step(0, 0, score=False, value=False)
            step(0, 1, value=False)
            step(0, 2)
            step(0, 3)
            with dve.Fori(1, H) as h:
                for k in range(B):
                    step(h, k)
            step(H, 0, proj=False, batch0_done=True)
            for i in range(NT):
                turned_tile("M", 0, i, TURNS + i)
            dve.wait_ge(gu_hi, 1)
            lower(gu_w[0][1][:, DT * I:], first_up, f32(gu_w[0][0][:, DT * I:])).then_inc(gu_lo, 1)
            step(H, 1, proj=False, score=False)

            def expert_step(it, k, up=True, down=True, more=True):
                def inner(j):
                    if not up:
                        return
                    g = (IT * k + j) % 2
                    need_e(dve, silu_ready, IT, it, k, j + 1)
                    need_e(dve, u_mm, IT, it, k, j + 1)
                    need_e(dve, h_lo, IT, it, k, j - 1)
                    nc.vector.tensor_tensor(prob[0:IW[j], 2 + g, :], t_bank[g][0:IW[j], :], prob[0:IW[j], g, :],
                                            ALU.mult).then_inc(h_ready, 1)

                def add(t):
                    if not down:
                        return
                    e = k - 1
                    need_e(dve, d_mm, NT, it, e, t + 1)
                    here = x_sb[:, 0, t, :]
                    at = it * 2 + e
                    factor = share[:, t, at:at + 1] if isinstance(at, int) else share[:, t, bass.ds(at, 1)]
                    nc.vector.scalar_tensor_tensor(out=here, in0=w_bank[t % 2][:], scalar=factor, in1=here,
                                                   op0=ALU.mult, op1=ALU.add).then_inc(y_added, 1)

                def gate_up_lo(half):
                    if not more:
                        return
                    e = k + 1
                    if half == 0:
                        need_e(dve, gu_hi, 1, it, e, 1)
                    hi, lo = [a[:, half * DT * I:(half + 1) * DT * I] for a in gu_w[e % 2]]
                    lower(lo, gu_stage[:, half * DT * I:(half + 1) * DT * I], f32(hi)).then_inc(gu_lo, 1)

                inner(0)
                add(0)
                add(1)
                inner(1)
                gate_up_lo(0)
                add(2)
                gate_up_lo(1)
                inner(2)
                add(3)

            expert_step(0, 0, down=False)
            expert_step(0, 1)
            with dve.Fori(1, E // 2 - 1) as it:
                expert_step(it, 0)
                expert_step(it, 1)
            expert_step(E // 2 - 1, 0)
            expert_step(E // 2 - 1, 1, more=False)
            expert_step(E // 2, 0, up=False, more=False)

        @block.gpsimd
        def _(pool):
            done = [0]

            def then_wait(ins):
                done[0] += 1
                ins.then_inc(pool_own, 1)
                pool.wait_ge(pool_own, done[0])

            def lower(dst, src, hi):
                return nc.gpsimd.tensor_tensor(dst, src, hi, ALU.subtract)

            def inverse_deviations(n, b):
                pool.wait_ge(moments, NT * (n + 1))
                wait(pool, rstd_ready, n)
                nc.gpsimd.tensor_tensor(var_eps[:], mean_var[:, b, :, 1], eps[:], ALU.add).then_inc(var_ready, 1)
                pool.wait_ge(var_ready, n + 1)
                nc.gpsimd.tensor_tensor(rstd[:, b, :], var_eps[:], minus_half[:], ALU.pow).then_inc(
                    rstd_ready, 1)

            nc.gpsimd.memset(ident[:], 0.0).then_inc(ident_ready, 1)
            pool.wait_ge(ident_ready, 1)
            nc.gpsimd.affine_select(out=ident[:], in_=ident[:], compare_op=ALU.not_equal, fill=1.0, base=0,
                                    pattern=[[-1, P]], channel_multiplier=1).then_inc(ident_ready, 1)
            pool.wait_ge(const_ready, 3)
            for kind, b in POOL_ORDER:
                if kind == "K" and b >= 2:
                    pool.wait_ge(split_hi, b + 1)
                    pool.wait_ge(split_lo, b)
                    hi, lo = [t[:, b - 1, :, :] for t in cT]
                    lower(lo, split_stage[b], f32(hi)).then_inc(split_lo, 1)
                elif kind in "mCE":
                    inverse_deviations(MOMENTS[kind, b] // NT, b)
                elif kind == "B":
                    pool.wait_ge(turned_lo, TURN["R", 0] + 1)
                    pool.wait_ge(xn_ready, XN["d", b] + NT)
                    for i in range(NT):
                        nc.gpsimd.tensor_tensor(x_sb[:, b, i, :], x_sb[:, b, i, :], bias_t,
                                                ALU.add).then_inc(bias_added, 1)
                elif kind == "G":
                    at = 2 * (b % 2)
                    pool.wait_ge(bit_tanh, b + 1)
                    nc.gpsimd.tensor_tensor(stage[:, at, :], stage[:, at, :], stage[:, at + 1, :],
                                            ALU.subtract).then_inc(bit_diff, 1)
                elif kind == "W":
                    pool.wait_ge(wf_hi, b + 1)
                    lower(wf[1][:, b, :], bit_acc, f32(wf[0][:, b, :])).then_inc(wf_lo, 1)

            def lower_weights(dst, slot, h, hi_done, lo_done):
                hi, lo = dst
                wait(pool, hi_done, h + 1)
                lower(lo, stage[:, slot, :], f32(hi)).then_inc(lo_done, 1)

            k_own = sem("k_own")

            def query_scale(h, u):
                need(pool, q_ss_out, 1, h, u, 1)
                nc.gpsimd.tensor_tensor(q_scale[:, u % 2, :], q_ss[:, u % 2, :], minus_half[:],
                                        ALU.pow).then_inc(q_scale_ready, 1)

            def step(h, k, score=True):
                if k == 0:
                    lower_weights([t[:, :, :].rearrange("p a c -> p (a c)") for t in wkv], 0, h, wkv_hi, wkv_lo)
                if score:
                    query_scale(h, k - 1)
                if k == 0:
                    lower_weights([t[:] for t in wq], 1, h, wq_hi, wq_lo)
                if k == 2:
                    lower_weights([t[:] for t in wo], 2, h, wo_hi, wo_lo)
                need(pool, k_squares, 4, h, k, 4)
                nc.gpsimd.tensor_tensor(k_ms[:], k_ss[:], eps[:], ALU.add).then_inc(k_own, 1)
                need(pool, k_own, 2, h, k, 1)
                nc.gpsimd.tensor_tensor(k_rs[:], k_ms[:], minus_half[:], ALU.pow).then_inc(k_own, 1)
                need(pool, k_own, 2, h, k, 2)
                keys = kv_raw[:, :, 0:HD]
                nc.gpsimd.tensor_tensor(keys, keys, k_rs[:].unsqueeze(2).to_broadcast([P, NT, HD]),
                                        ALU.mult).then_inc(k_scaled, 1)
                hi, lo = [t[:, k % 2, 1, :].rearrange("p (j c) -> p j c", j=NT) for t in kv]
                need(pool, v_hi, 1, h, k, 1)
                lower(lo, kv_raw[:, :, HD:2 * HD], f32(hi)).then_inc(v_lo, 1)
                need(pool, q_squared, 2, h, k, 2)
                lower(sqs[1][:], sq[:], f32(sqs[0][:])).then_inc(sq_lo, 1)

            step(0, 0, score=False)
            for k in range(1, B):
                step(0, k)
            with pool.Fori(1, H) as h:
                for k in range(B):
                    step(h, k)
            query_scale(H, -1)
            inverse_deviations(NMOMENTS // NT, 0)
            pool.wait_ge(gate_hi, 1)
            lower(gu_w[0][1][:, 0:DT * I], first_gate, f32(gu_w[0][0][:, 0:DT * I])).then_inc(gu_lo, 1)

            def expert_step(it, k):
                def inner_lo(j):
                    need_e(pool, h_hi, IT, it, k, j + 1)
                    lower(hT[k % 2][1][0:IW[j], j, :], prob[0:IW[j], 2 + (IT * k + j) % 2, :],
                          f32(hT[k % 2][0][0:IW[j], j, :])).then_inc(h_lo, 1)

                need_e(pool, dn_hi, 1, it, k, 1)
                lower(dn_w[k % 2][1], dn_stage, f32(dn_w[k % 2][0])).then_inc(dn_lo, 1)
                inner_lo(0)
                inner_lo(1)
                inner_lo(2)

            expert_step(0, 0)
            expert_step(0, 1)
            with pool.Fori(1, E // 2) as it:
                expert_step(it, 0)
                expert_step(it, 1)


def kernel(**inputs):
    import numpy as np
    import concourse.bacc as bacc
    from concourse.bass_utils import run_bass_kernel_spmd

    a = {name: np.asarray(value) for name, value in inputs.items()}

    def whole(v):
        return np.ascontiguousarray(v)

    ctxT = a["ctx_1024"].transpose(0, 2, 1).reshape(B, CT, P, S)
    columns = [a["L0_xattn_bq"], a["L0_xattn_bk"], a["L1_xattn_gq"], a["L1_xattn_gk"]]
    for name in ("g_xattn", "g_ffn", "L0_ffn_exps", "L0_ffn_bexps", "L0_ffn_mask_weight", "L0_ffn_scale",
                 "L0_ffn_biasscale"):
        columns += [np.broadcast_to(v, (P,)) for v in a[name]]
    columns += [a[n].reshape(DT, P, NBITS)[j, :, bit] for n in ("L0_ffn_pbias", "L0_ffn_nbias")
                for bit in range(NBITS) for j in range(DT)]
    vecs = np.stack(columns, axis=1)
    w0 = np.stack([a[n].T.reshape(CT, P, P).transpose(1, 0, 2) for n in ("L0_xattn_Wq", "L0_xattn_Wk")], axis=1)
    bits = np.stack([a[n].transpose(2, 1, 0).reshape(NBITS, DT, P, D) for n in ("L0_ffn_pweight", "L0_ffn_nweight")],
                    axis=2).transpose(1, 0, 2, 3, 4).reshape(DT * NBITS, 2, P, D)
    wk, wv = (a[n].reshape(CT, P, H, HD).transpose(2, 1, 0, 3) for n in ("L1_xattn_Wk", "L1_xattn_Wv"))
    wkv = np.stack([wk, wv], axis=3).reshape(H, P, CT * 2 * HD)
    wq = a["L1_xattn_Wq"].reshape(DT, P, H, HD).transpose(2, 1, 0, 3).reshape(H, P, DT * HD)
    w1 = np.stack([wkv, wq, a["L1_xattn_Wo"].reshape(H, HD, D)], axis=0)
    w_gu = np.stack([a[n].transpose(0, 2, 1).reshape(E, DT, P, I).transpose(0, 2, 1, 3)
                     for n in ("L1_ffn_gate_weight", "L1_ffn_up_weight")], axis=2).reshape(E, P, 2 * DT * I)
    down = np.zeros((E, IT * P, D), a["L1_ffn_down_weight"].dtype)
    down[:, :I] = a["L1_ffn_down_weight"].transpose(0, 2, 1)
    w_dn = down.reshape(E, IT, P, D).transpose(0, 2, 1, 3).reshape(E, P, IT * D)

    def by_tile(v):
        return v.reshape(NT, P, TOPK).transpose(1, 0, 2)

    arrays = {
        "x": a["x"].reshape(B * S, D), "ctxT": ctxT, "vecs": vecs, "w0": w0.reshape(P, 2 * CT * P), "bits": bits,
        "w1": w1, "w_gu": w_gu, "w_dn": w_dn, "topk_idx": by_tile(a["L1_ffn_topk_idx"]),
        "topk_w": by_tile(a["L1_ffn_topk_weight"]),
    }
    arrays = {name: whole(v) for name, v in arrays.items()}
    nc = bacc.Bacc("TRN2", target_bir_lowering=False, num_devices=1, dynamic_dma_scratch_size=4096)
    args = [nc.dram_tensor(name, v.shape, mybir.dt.from_np(v.dtype), kind="ExternalInput").ap()
            for name, v in arrays.items()]
    out = nc.dram_tensor("out", (B * S, D), F32, kind="ExternalOutput").ap()
    flamingo_kernel(nc, *args, out)
    result = run_bass_kernel_spmd(nc, [arrays], core_ids=[0])
    return result.results[0]["out"].reshape(B, S, D)
```
